# Optimizing a Trainium2 kernel written in Bass

```python
import numpy as np
import jax
import jax.numpy as jnp

def _softmax(x, axis=-1):
    return jax.nn.softmax(x, axis=axis)

def _gelu(x):
    return jax.nn.gelu(x, approximate=True)

def _silu(x):
    return jax.nn.silu(x)

def _sigmoid(x):
    return jax.nn.sigmoid(x)

def _layernorm(x, axis=-1, eps=1e-05):
    m = jnp.mean(x, axis=axis, keepdims=True)
    v = jnp.var(x, axis=axis, keepdims=True)
    return (x - m) / jnp.sqrt(v + eps)

def _scatter_add(tgt, idx, src, axis=0):
    return tgt.at[idx].add(src)

def _segment_sum(src, seg, n):
    return jax.ops.segment_sum(src, seg, n)
kernel_name = 'mk_adaln_attn_ffn_d1_seqx_r4_2ea6de'

def setup_inputs(seed: int=0):
    np.random.seed(seed)
    _w = jnp.asarray

    def _rec_inputs():
        import jax
        import jax.numpy as jnp
        _rk = jax.random.key(seed)
        x = -0.000125 + 0.9999 * jax.random.normal(jax.random.fold_in(_rk, 1), (8, 256, 1024), jnp.float32)
        _lenS = 256 - jax.random.randint(jax.random.fold_in(_rk, 7), (8,), 0, max(1, 256 // 4) + 1, jnp.int32)
        _lenS2 = 256 - jax.random.randint(jax.random.fold_in(_rk, 8), (8,), 0, max(1, 256 // 4) + 1, jnp.int32)
        itok_B_0_23 = jax.random.randint(jax.random.fold_in(_rk, 11), (8,), 0, 24, jnp.int32)
        itok_B_3_7 = jax.random.randint(jax.random.fold_in(_rk, 12), (8,), 3, 8, jnp.int32)
        return (x, itok_B_0_23, itok_B_3_7)
    x, itok_B_0_23, itok_B_3_7 = _rec_inputs()

    def _L0_cond_setup():
        import jax, jax.numpy as jnp
        import numpy as np
        R = 16
        ALPHA = 32
        SCALING = ALPHA / R
        SLOTS = 32
        IN_F = 1024
        OUT_F = 1024
        B, T = (8, 256)
        key = jax.random.key(seed)
        k1, k2, k3, k4, k5, k6 = jax.random.split(key, 6)
        x = jax.random.normal(k1, (B, T, IN_F), dtype=jnp.float32)
        adapter_mapping = jax.random.randint(k2, (B,), 0, SLOTS, dtype=jnp.int32)
        W = jax.random.normal(k3, (OUT_F, IN_F), dtype=jnp.float32) * 0.02
        b = jax.random.normal(k4, (OUT_F,), dtype=jnp.float32) * 0.02
        lora_As = jax.random.normal(k5, (SLOTS, IN_F, R), dtype=jnp.float32) * 0.02
        lora_Bs = jax.random.normal(k6, (SLOTS, R, OUT_F), dtype=jnp.float32) * 0.02
        return {'x': x, 'adapter_mapping': adapter_mapping, 'W': W, 'b': b, 'lora_As': lora_As, 'lora_Bs': lora_Bs}
    _L0_cond_all = _L0_cond_setup()
    _L0_cond_in = {k: v for k, v in _L0_cond_all.items() if k in ('W', 'b', 'lora_As', 'lora_Bs')}
    del _L0_cond_all

    def _L0_attn_setup():
        import jax, jax.numpy as jnp
        import numpy as np
        NUM_HEAD = 32
        NUM_KV = 8
        HIDDEN = 1024
        HEAD_DIM = HIDDEN // NUM_HEAD
        KV_DIM = HEAD_DIM * NUM_KV
        key = jax.random.key(seed)
        ks = jax.random.split(key, 5)
        bs, seq = (2, 512)
        scale = 0.02
        return {'x': jax.random.normal(ks[0], (bs, seq, HIDDEN), dtype=jnp.float32), 'w_q': jax.random.normal(ks[1], (HIDDEN, HIDDEN), dtype=jnp.float32) * scale, 'w_k': jax.random.normal(ks[2], (HIDDEN, KV_DIM), dtype=jnp.float32) * scale, 'w_v': jax.random.normal(ks[3], (HIDDEN, KV_DIM), dtype=jnp.float32) * scale, 'w_o': jax.random.normal(ks[4], (HIDDEN, HIDDEN), dtype=jnp.float32) * scale}
    _L0_attn_all = _L0_attn_setup()
    _L0_attn_in = {k: v for k, v in _L0_attn_all.items() if k in ('w_q', 'w_k', 'w_v', 'w_o')}
    del _L0_attn_all

    def _L0_cond2_setup():
        import jax, jax.numpy as jnp
        import numpy as np
        MAX_LORAS, OUT, IN = (8, 1024, 1024)
        B, S = (4, 512)
        key = jax.random.key(seed)
        k1, k2, k3 = jax.random.split(key, 3)
        x = jax.random.normal(k1, (B, S, IN), dtype=jnp.float32)
        weight = jax.random.normal(k2, (MAX_LORAS, OUT, IN), dtype=jnp.float32) * 0.02
        adapter_ids = jax.random.randint(k3, (B,), 0, MAX_LORAS, dtype=jnp.int32)
        return {'x': x, 'weight': weight, 'adapter_ids': adapter_ids}
    _L0_cond2_all = _L0_cond2_setup()
    _L0_cond2_in = {k: v for k, v in _L0_cond2_all.items() if k in ('weight',)}
    del _L0_cond2_all

    def _L0_ffn_setup():
        import jax, jax.numpy as jnp
        import numpy as np
        LORA_SCALE = 16.0 / jnp.sqrt(16.0)
        TOP_K = 2
        key = jax.random.key(seed)
        k1, k2, k3, k4 = jax.random.split(key, 4)
        B_, S, D, O, E, R = (4, 512, 1024, 1024, 4, 16)
        x = jax.random.normal(k1, (B_, S, D), dtype=jnp.float32)
        router_w = jax.random.normal(k2, (E, D), dtype=jnp.float32) * 0.02
        A = jax.random.normal(k3, (E, R, D), dtype=jnp.float32) * 0.02
        B = jax.random.normal(k4, (O,), dtype=jnp.float32)
        B = jax.random.normal(k4, (E, O, R), dtype=jnp.float32) * 0.02
        return {'x': x, 'router_w': router_w, 'A': A, 'B': B}
    _L0_ffn_all = _L0_ffn_setup()
    _L0_ffn_in = {k: v for k, v in _L0_ffn_all.items() if k in ('router_w', 'A', 'B')}
    del _L0_ffn_all
    return {'x': x, 'itok_B_0_23': itok_B_0_23, 'itok_B_3_7': itok_B_3_7, 'L0_cond_W': _L0_cond_in['W'], 'L0_cond_b': _L0_cond_in['b'], 'L0_cond_lora_As': _L0_cond_in['lora_As'], 'L0_cond_lora_Bs': _L0_cond_in['lora_Bs'], 'L0_attn_w_q': _L0_attn_in['w_q'], 'L0_attn_w_k': _L0_attn_in['w_k'], 'L0_attn_w_v': _L0_attn_in['w_v'], 'L0_attn_w_o': _L0_attn_in['w_o'], 'L0_cond2_weight': _L0_cond2_in['weight'], 'L0_ffn_router_w': _L0_ffn_in['router_w'], 'L0_ffn_A': _L0_ffn_in['A'], 'L0_ffn_B': _L0_ffn_in['B']}

def reference(x, itok_B_0_23, itok_B_3_7, L0_cond_W, L0_cond_b, L0_cond_lora_As, L0_cond_lora_Bs, L0_attn_w_q, L0_attn_w_k, L0_attn_w_v, L0_attn_w_o, L0_cond2_weight, L0_ffn_router_w, L0_ffn_A, L0_ffn_B):
    import jax
    import jax.numpy as jnp

    def _L0_cond_ref(x, adapter_mapping, W, b, lora_As, lora_Bs):
        import jax, jax.numpy as jnp
        import numpy as np
        R = 16
        ALPHA = 32
        SCALING = ALPHA / R
        SLOTS = 32
        IN_F = 1024
        OUT_F = 1024
        B, T = (8, 256)
        base_out = jnp.einsum('bti,oi->bto', x, W) + b
        A = lora_As[adapter_mapping]
        Bm = lora_Bs[adapter_mapping]
        lora_h = jnp.einsum('bti,bir->btr', x, A)
        lora_out = jnp.einsum('btr,bro->bto', lora_h, Bm)
        return base_out + lora_out * SCALING

    def _L0_attn_ref(x, w_q, w_k, w_v, w_o):
        import jax, jax.numpy as jnp
        import numpy as np
        NUM_HEAD = 32
        NUM_KV = 8
        HIDDEN = 1024
        HEAD_DIM = HIDDEN // NUM_HEAD
        KV_DIM = HEAD_DIM * NUM_KV
        bs, seq, _ = x.shape
        group = NUM_HEAD // NUM_KV
        q = (x @ w_q).reshape(bs, seq, NUM_HEAD, HEAD_DIM).transpose(0, 2, 1, 3)
        k = (x @ w_k).reshape(bs, seq, NUM_KV, HEAD_DIM).transpose(0, 2, 1, 3)
        v = (x @ w_v).reshape(bs, seq, NUM_KV, HEAD_DIM).transpose(0, 2, 1, 3)
        k = jnp.repeat(k, group, axis=1)
        v = jnp.repeat(v, group, axis=1)
        scores = jnp.einsum('bhqd,bhkd->bhqk', q, k) / jnp.sqrt(jnp.float32(HEAD_DIM))
        weights = jax.nn.softmax(scores, axis=-1)
        o = jnp.einsum('bhqk,bhkd->bhqd', weights, v)
        o = o.transpose(0, 2, 1, 3).reshape(bs, seq, HIDDEN)
        return o @ w_o

    def _L0_cond2_ref(x, weight, adapter_ids):
        import jax, jax.numpy as jnp
        import numpy as np
        MAX_LORAS, OUT, IN = (8, 1024, 1024)
        B, S = (4, 512)
        w = weight[adapter_ids]
        return jnp.einsum('bsi,boi->bso', x, w)

    def _L0_ffn_ref(x, router_w, A, B):
        import jax, jax.numpy as jnp
        import numpy as np
        LORA_SCALE = 16.0 / jnp.sqrt(16.0)
        TOP_K = 2
        D = x.shape[-1]
        flat = x.reshape(-1, D)
        logits = flat @ router_w.T
        topk_vals, topk_idx = jax.lax.top_k(logits, TOP_K)
        sparse = jnp.full_like(logits, -jnp.inf)
        rows = jnp.arange(logits.shape[0])[:, None]
        sparse = sparse.at[rows, topk_idx].set(topk_vals)
        gates = jax.nn.softmax(sparse, axis=-1)
        mid = jnp.einsum('tf,erf->ter', flat, A)
        all_deltas = jnp.einsum('ter,eor->teo', mid, B) * LORA_SCALE
        delta = jnp.einsum('te,teo->to', gates, all_deltas)
        return delta.reshape(*x.shape[:-1], -1)
    x = x + _L0_attn_ref(_L0_cond_ref(x, itok_B_0_23, L0_cond_W, L0_cond_b, L0_cond_lora_As, L0_cond_lora_Bs), L0_attn_w_q, L0_attn_w_k, L0_attn_w_v, L0_attn_w_o)
    x = x + _L0_ffn_ref(_L0_cond2_ref(x, L0_cond2_weight, itok_B_3_7), L0_ffn_router_w, L0_ffn_A, L0_ffn_B)
    return x

_drawn_inputs = setup_inputs


def setup_inputs(seed=0):
    import zlib

    import numpy as np

    out = dict(_drawn_inputs(seed))
    spreads = {}
    factors = {'L0_cond_W': 3.076,
     'L0_cond_b': 6.037,
     'L0_cond_lora_As': 8.0,
     'L0_cond_lora_Bs': 8.0,
     'L0_attn_w_q': 8.0,
     'L0_attn_w_k': 8.0,
     'L0_attn_w_v': 2.695,
     'L0_attn_w_o': 2.871}
    for name, (base, spread) in spreads.items():
        noise = np.random.default_rng([zlib.crc32(name.encode()), seed]).standard_normal(out[name].shape)
        drawn = base * np.exp(spread * noise) if base else spread * noise
        out[name] = jnp.asarray(drawn.astype(out[name].dtype))
    for name, factor in factors.items():
        out[name] = (out[name] * factor).astype(out[name].dtype)
    return out
```

```python
from contextlib import ExitStack

import numpy as np

import concourse.bass as bass
from concourse import mybir

P = 128
B, T, D = 8, 256, 1024
KT = D // P
H, G, HD = 32, 8, 32
HG = H // G
NKV = G * HD
NQKV = D + 2 * NKV
R = 16
LORA_SCALE = 2.0
E = 4
ER = E * R
EC = ER + E
FFN_SCALE = 4.0
T2 = 2 * T
PAIRS = B // 2
ATT_SCALE = float(HD) ** -0.5

F32 = mybir.dt.float32
F32R = mybir.dt.float32r
I32 = mybir.dt.int32
ACT = mybir.ActivationFunctionType
ALU = mybir.AluOpType
AX = mybir.AxisListType


def f(ap):
    return ap.bitcast(F32)


def project_tokens(nc, xT, idx, WT, bias, lora_A, lora_B, hT):
    H_BANKS = 4
    SLOTS = 4
    LANDED = 2 * (1 + 1 + 3)
    with ExitStack() as ctx:
        def sb(name, shape, dt=F32):
            return ctx.enter_context(nc.sbuf_tensor(name, shape, dt))

        def psum(name, shape):
            return ctx.enter_context(nc.psum_tensor(name, shape, F32))

        def sem(name):
            return ctx.enter_context(nc.semaphore(name))

        idx_sb = sb("idx_sb", [1, B], I32)
        bias_sb = sb("bias_sb", [P, KT])
        w_raw = sb("w_raw", [P, 2, D])
        w_hi, w_lo = sb("w_hi", [P, KT, D], F32R), sb("w_lo", [P, KT, D], F32R)
        x_raw = sb("x_raw", [P, 2, KT, T2])
        x_hi, x_lo = sb("x_hi", [P, KT, T2], F32R), sb("x_lo", [P, KT, T2], F32R)
        a_raw = sb("a_raw", [P, 2, 2, KT, R])
        a_hi, a_lo = sb("a_hi", [P, 2, KT, R], F32R), sb("a_lo", [P, 2, KT, R], F32R)
        b_raw = sb("b_raw", [96, 2, 2, D])
        b_stack = sb("b_stack", [96, 2, D], F32R)
        b_top = sb("b_top", [96, 2, D], F32R)
        u_stack = sb("u_stack", [96, 2, T], F32R)
        h_out = sb("h_out", [P, SLOTS, T2])
        psU = psum("psU", [P, 512])
        psH = psum("psH", [P, H_BANKS, T2])

        idx_landed, bias_landed = sem("idx_landed"), sem("bias_landed")
        w_landed = [sem(f"w_landed{i}") for i in range(2)]
        in_landed = [sem(f"in_landed{i}") for i in range(2)]
        w_hi_done, w_lo_done = sem("w_hi_done"), sem("w_lo_done")
        zeroed = sem("zeroed")
        x_hi_done, x_lo_done = sem("x_hi_done"), sem("x_lo_done")
        ab_hi_done, ab_lo_done = sem("ab_hi_done"), sem("ab_lo_done")
        b_top_done = sem("b_top_done")
        u_done, u_hi_done, u_lo_done = sem("u_done"), sem("u_hi_done"), sem("u_lo_done")
        h_done, h_copied = sem("h_done"), sem("h_copied")
        h_stored = [sem(f"h_stored{i}") for i in range(SLOTS)]
        block = ctx.enter_context(nc.Block())

        @block.sync
        def _(sp):
            for s in range(SLOTS):
                sp.sem_inc(h_stored[s], 16)
            sp.dma_start(idx_sb[:], idx).then_inc(idx_landed, 16)
            sp.dma_start(bias_sb[:], bias).then_inc(bias_landed, 16)

            def load_pair(pair, j):
                for c in range(2):
                    sp.dma_start(x_raw[:, j, :, c * T:(c + 1) * T],
                                 xT[bass.ds(2 * pair + c, 1)].rearrange("b p k t -> p (b k) t")
                                 ).then_inc(in_landed[j], 16)
                    slot = sp.value_load(idx_sb[0:1, bass.ds(2 * pair + c, 1)], min_val=0, max_val=31)
                    sp.dma_start(a_raw[:, j, c], lora_A[bass.ds(slot, 1)].rearrange("s p k r -> p (s k) r")
                                 ).then_inc(in_landed[j], 16)
                    for q in range(3):
                        sp.dma_start(b_raw[32 * q:32 * q + R, j, c],
                                     lora_B[bass.ds(slot, 1)].rearrange("s r d -> (s r) d")
                                     ).then_inc(in_landed[j], 16)

            def load_w(k):
                if k >= 2:
                    sp.wait_ge(w_lo_done, k - 1)
                sp.dma_start(w_raw[:, k % 2], WT[:, k]).then_inc(w_landed[k % 2], 16)

            load_w(0)
            sp.wait_ge(idx_landed, 16)
            load_pair(0, 0)
            for k in range(1, KT):
                load_w(k)
            load_pair(1, 1)

            def store_pair(pair):
                for m in range(KT):
                    sp.wait_ge(h_copied, KT * pair + m + 1 + H_BANKS)
                    sp.dma_start(hT[bass.ds(2 * pair, 2), :, m].rearrange("b p t -> p b t"),
                                 h_out[:, m % SLOTS].rearrange("p (b t) -> p b t", b=2)
                                 ).then_inc(h_stored[m % SLOTS], 16)

            with sp.Fori(0, PAIRS // 2 - 1) as pp:
                for j in range(2):
                    sp.wait_ge(x_lo_done, 2 * pp + j + 1)
                    sp.wait_ge(ab_lo_done, 2 * pp + j + 1)
                    load_pair(2 * pp + j + 2, j)
                    store_pair(2 * pp + j)
            store_pair(PAIRS - 2)
            store_pair(PAIRS - 1)
            for s in range(SLOTS):
                sp.wait_ge(h_stored[s], 16 * (1 + PAIRS * KT // SLOTS))

        @block.scalar
        def _(act):
            act.sem_inc(h_copied, H_BANKS)
            act.wait_ge(bias_landed, 16)

            def split_w_hi(k):
                act.wait_ge(w_landed[k % 2], 16 * (k // 2 + 1))
                nc.scalar.activation(w_hi[:, k], w_raw[:, k % 2], ACT.Copy).then_inc(w_hi_done, 1)

            for k in range(KT):
                split_w_hi(k)
            act.wait_ge(zeroed, 2)
            with act.Fori(0, PAIRS // 2) as pp:
                for j in range(2):
                    pair = 2 * pp + j
                    act.wait_ge(in_landed[j], 16 * LANDED * (pp + 1))
                    nc.scalar.activation(a_hi[:], a_raw[:, j], ACT.Copy).then_inc(ab_hi_done, 1)
                    for c in range(2):
                        for q in (0, 2):
                            nc.scalar.activation(b_stack[32 * q:32 * q + R, c],
                                                 b_raw[32 * q:32 * q + R, j, c], ACT.Copy).then_inc(ab_hi_done, 1)
                        nc.scalar.activation(b_top[32:32 + R, c], b_raw[32:32 + R, j, c],
                                             ACT.Copy).then_inc(b_top_done, 1)
                    nc.scalar.activation(x_hi[:], x_raw[:, j], ACT.Copy).then_inc(x_hi_done, 1)
                    act.wait_ge(u_done, pair + 1)
                    u = psU[0:R, :].rearrange("p (b t) -> p b t", b=2)
                    for q in (0, 1):
                        nc.scalar.activation(u_stack[32 * q:32 * q + R], u, ACT.Copy,
                                             scale=LORA_SCALE).then_inc(u_hi_done, 1)
                    for m in range(KT):
                        act.wait_ge(h_done, KT * pair + m + 1)
                        act.wait_ge(h_stored[m % SLOTS], 16 * (2 * pair + m // SLOTS + 1))
                        nc.scalar.activation(h_out[:, m % SLOTS], psH[:, m % H_BANKS], ACT.Identity,
                                             bias=bias_sb[:, m:m + 1]).then_inc(h_copied, 1)

        @block.vector
        def _(dve):
            dve.memset(f(b_stack[:]), 0.0).then_inc(zeroed, 1)
            dve.memset(f(u_stack[:]), 0.0).then_inc(zeroed, 1)
            for k in range(KT):
                dve.wait_ge(w_hi_done, k + 1)
                dve.tensor_tensor(w_lo[:, k], w_raw[:, k % 2], f(w_hi[:, k]), ALU.subtract).then_inc(w_lo_done, 1)
            with dve.Fori(0, PAIRS // 2) as pp:
                for j in range(2):
                    pair = 2 * pp + j
                    dve.wait_ge(ab_hi_done, 5 * pair + 5)
                    dve.wait_ge(b_top_done, 2 * pair + 2)
                    for c in range(2):
                        dve.tensor_tensor(b_stack[32:32 + R, c], b_raw[32:32 + R, j, c],
                                          f(b_top[32:32 + R, c]), ALU.subtract)
                    dve.tensor_tensor(a_lo[:], a_raw[:, j], f(a_hi[:]), ALU.subtract).then_inc(ab_lo_done, 1)
                    dve.wait_ge(x_hi_done, pair + 1)
                    dve.tensor_tensor(x_lo[:], x_raw[:, j], f(x_hi[:]), ALU.subtract).then_inc(x_lo_done, 1)
                    dve.wait_ge(u_hi_done, 2 * pair + 2)
                    dve.scalar_tensor_tensor(u_stack[64:64 + R], psU[0:R, :].rearrange("p (b t) -> p b t", b=2),
                                             LORA_SCALE, f(u_stack[0:R]), ALU.mult, ALU.subtract).then_inc(u_lo_done, 1)

        @block.tensor
        def _(pe):
            pe.wait_ge(w_lo_done, KT)
            with pe.Fori(0, PAIRS) as pair:
                pe.wait_ge(ab_lo_done, pair + 1)
                pe.wait_ge(x_lo_done, pair + 1)
                for c in range(2):
                    n = 0
                    for k in range(KT):
                        for a, x in ((a_hi, x_hi), (a_hi, x_lo), (a_lo, x_hi)):
                            mm = pe.matmul(psU[0:R, c * T:(c + 1) * T], a[:, c, k], x[:, k, c * T:(c + 1) * T],
                                           start=(n == 0), stop=(n == 3 * KT - 1))
                            n += 1
                mm.then_inc(u_done, 1)
                for m in range(KT):
                    pe.wait_ge(h_copied, KT * pair + m + 1)
                    out = psH[:, m % H_BANKS]
                    cols = slice(m * P, (m + 1) * P)
                    n = 0
                    for k in range(KT):
                        for w, x in ((w_hi, x_hi), (w_hi, x_lo), (w_lo, x_hi)):
                            pe.matmul(out, w[:, k, cols], x[:, k], start=(n == 0), stop=False)
                            n += 1
                    if m == 0:
                        pe.wait_ge(u_lo_done, pair + 1)
                    for c in range(2):
                        mm = pe.matmul(out[:, c * T:(c + 1) * T], b_stack[:, c, cols], u_stack[:, c],
                                       start=False, stop=(c == 1))
                    mm.then_inc(h_done, 1)


def attend(nc, hT, Wqkv, ident, oT, den):
    KK = 2
    STEPS = G + 3
    UNITS = 4 + G
    TILES = 4
    with ExitStack() as ctx:
        def sb(name, shape, dt=F32):
            return ctx.enter_context(nc.sbuf_tensor(name, shape, dt))

        def psum(name, shape):
            return ctx.enter_context(nc.psum_tensor(name, shape, F32))

        def sem(name):
            return ctx.enter_context(nc.semaphore(name))

        id_sb = sb("id_sb", [P, P])
        w_raw = sb("wq_raw", [P, 2, NQKV])
        w_hi, w_lo = sb("wq_hi", [P, KT, NQKV], F32R), sb("wq_lo", [P, KT, NQKV], F32R)
        h_raw = sb("h_raw", [P, KT, T])
        h_hi, h_lo = sb("h_hi", [P, KT, T], F32R), sb("h_lo", [P, KT, T], F32R)
        k_stack = sb("k_stack", [98, G, T], F32R)
        q_stack = sb("q_stack", [98, 4, HG, T], F32R)
        v_pad = sb("v_pad", [P, KK, G, 5 * HD])
        nmax = sb("nmax", [P, 2, HG, 2])
        nmax_parts = sb("nmax_parts", [P, 2, 2 * HG * 2], F32R)
        nmax_rows = sb("nmax_rows", [2 * HG * 2, 2, P])
        probs = sb("probs", [P, 2, KK, HG * T])
        o_sb = sb("o_sb", [P, G, T])
        den_sb = sb("den_sb", [P, G, 2, T])

        psP = psum("psP", [P, 2, 512])
        psS = psum("psS", [P, 2, 512])
        psT = psum("psT", [P, 2, 512])
        psO = psum("psO", [P, 2, T])
        psM = psum("psM", [P, P])

        id_landed = sem("id_landed2")
        w_landed = [sem(f"wq_landed{i}") for i in range(2)]
        w_hi_done, w_lo_done = sem("wq_hi_done"), sem("wq_lo_done")
        filled = sem("filled")
        h_landed, h_hi_done, h_lo_done = sem("h_landed"), sem("h_hi_done"), sem("h_lo_done")
        proj_done = sem("proj_done")
        proj_act, proj_dve = sem("proj_act"), sem("proj_dve")
        s_done, s_max = sem("s_done"), sem("s_max")
        nmax_hi, nmax_lo = sem("nmax_hi"), sem("nmax_lo")
        turned, rows_done, rows_landed = sem("turned"), sem("rows_done"), sem("rows_landed")
        st_done, exp_done = sem("st_done"), sem("exp_done")
        pv_done, o_copied, o_stored = sem("pv_done"), sem("o_copied"), sem("o_stored")
        block = ctx.enter_context(nc.Block())

        @block.sync
        def _(sp):
            sp.sem_inc(o_stored, 48)
            sp.dma_start(id_sb[:], ident).then_inc(id_landed, 16)
            sp.dma_start(h_raw[:], hT[0]).then_inc(h_landed, 16)
            for k in range(KT):
                if k >= 2:
                    sp.wait_ge(w_lo_done, k - 1)
                sp.dma_start(w_raw[:, k % 2], Wqkv[k * P:(k + 1) * P]).then_inc(w_landed[k % 2], 16)

            def batch(b, last):
                if not last:
                    sp.wait_ge(h_lo_done, b + 1)
                    sp.dma_start(h_raw[:], hT[bass.ds(b + 1, 1)].rearrange("b p k t -> p (b k) t")
                                 ).then_inc(h_landed, 16)
                for g in range(G):
                    sp.wait_ge(rows_done, G * b + g + 1)
                    for part in range(2):
                        sp.dma_start(f(q_stack[96 + part:97 + part, g % 4].rearrange("p h t -> p (h t)")),
                                     nmax_rows[8 * part:8 * part + 8, g % 2]).then_inc(rows_landed, 16)
                sp.wait_ge(o_copied, G * b + G + 1)
                sp.dma_start(oT[bass.ds(b, 1)].rearrange("b p g t -> p (b g) t"), o_sb[:]).then_inc(o_stored, 16)
                for parity in range(2):
                    sp.dma_start(den[bass.ds(b, 1), parity].rearrange("b g c t -> b (g c t)"),
                                 den_sb[64 + 32 * parity:65 + 32 * parity].rearrange("p g c t -> p (g c t)")
                                 ).then_inc(o_stored, 16)

            with sp.Fori(0, B - 1) as b:
                batch(b, False)
            batch(B - 1, True)
            sp.wait_ge(o_stored, 48 * (B + 1))

        @block.gpsimd
        def _(pool):
            pool.memset(v_pad[:], 0.0).then_inc(filled, 1)
            pool.wait_ge(filled, 1)
            pool.memset(v_pad[:, :, :, 3 * HD:4 * HD], 1.0).then_inc(filled, 1)
            pool.wait_ge(filled, 2)
            pool.memset(f(k_stack[96:98]), 1.0).then_inc(filled, 1)

        @block.scalar
        def _(act):
            act.sem_inc(exp_done, 2)
            for k in range(KT):
                act.wait_ge(w_landed[k % 2], 16 * (k // 2 + 1))
                nc.scalar.activation(w_hi[:, k], w_raw[:, k % 2], ACT.Copy).then_inc(w_hi_done, 1)

            def split_h(b):
                act.wait_ge(h_landed, 16 * b + 16)
                nc.scalar.activation(h_hi[:], h_raw[:], ACT.Copy).then_inc(h_hi_done, 1)

            def copy_k(b, j):
                act.wait_ge(proj_done, UNITS * b + j + 1)
                for i in range(4):
                    kv = 4 * j + i
                    for q in (0, 1):
                        ins = nc.scalar.activation(k_stack[32 * q:32 * q + 32, kv], psP[32 * i:32 * i + 32, j, 0:T],
                                                   ACT.Copy)
                ins.then_inc(proj_act, 1)

            def copy_v(b, t):
                act.wait_ge(proj_done, UNITS * b + 2 + t + 1)
                v = psP[:, t % 2, 0:NKV].rearrange("p (g d) -> p g d", g=G)
                nc.scalar.activation(v_pad[:, t, 0:4, HD:2 * HD], v[:, 0:4], ACT.Copy).then_inc(proj_act, 1)

            def copy_q(b, g):
                act.wait_ge(proj_done, UNITS * b + 4 + g + 1)
                for h in range(HG):
                    for q in (0, 2):
                        ins = nc.scalar.activation(q_stack[32 * q:32 * q + 32, g % 4, h],
                                                   psP[32 * h:32 * h + 32, g % 2, 0:T], ACT.Copy)
                ins.then_inc(proj_act, 1)

            def batch(b, last):
                for s in range(STEPS):
                    if s < G:
                        copy_q(b, s)
                    if s == G and not last:
                        act.wait_ge(proj_done, UNITS * (b + 1))
                        split_h(b + 1)
                    if 2 <= s < G + 2:
                        g = s - 2
                        for hp in range(2):
                            for kt in range(KK):
                                n = 2 * hp + kt
                                act.wait_ge(st_done, TILES * (G * b + g) + n + 1)
                                if n == 0 and g >= 2:
                                    act.wait_ge(pv_done, 2 * (G * b + g) - 2)
                                nc.scalar.activation(probs[:, g % 2, kt, hp * 512:(hp + 1) * 512], psT[:, n % 2],
                                                     ACT.Exp, scale=ATT_SCALE).then_inc(exp_done, 1)
                    if 1 <= s <= G:
                        g = s - 1
                        act.wait_ge(turned, G * b + g + 1)
                        nc.scalar.activation(nmax_rows[:, g % 2], psM[0:16, 0:P], ACT.Copy).then_inc(rows_done, 1)
                if not last:
                    for j in range(2):
                        copy_k(b + 1, j)
                    act.wait_ge(pv_done, 2 * G * b + 2 * G)
                    for t in range(2):
                        copy_v(b + 1, t)

            split_h(0)
            for j in range(2):
                copy_k(0, j)
            act.wait_ge(filled, 3)
            for t in range(2):
                copy_v(0, t)
            with act.Fori(0, B - 1) as b:
                batch(b, False)
            batch(B - 1, True)

        @block.vector
        def _(dve):
            dve.sem_inc(s_max, 2)
            dve.sem_inc(o_copied, 1)
            for k in range(KT):
                dve.wait_ge(w_hi_done, k + 1)
                dve.tensor_tensor(w_lo[:, k], w_raw[:, k % 2], f(w_hi[:, k]), ALU.subtract).then_inc(w_lo_done, 1)

            def split_h(b):
                dve.wait_ge(h_hi_done, b + 1)
                dve.tensor_tensor(h_lo[:], h_raw[:], f(h_hi[:]), ALU.subtract).then_inc(h_lo_done, 1)

            def copy_k(b, j):
                dve.wait_ge(proj_act, UNITS * b + j + 1)
                for i in range(4):
                    kv = 4 * j + i
                    ins = dve.tensor_tensor(k_stack[64:96, kv], psP[32 * i:32 * i + 32, j, 0:T],
                                            f(k_stack[0:32, kv]), ALU.subtract)
                ins.then_inc(proj_dve, 1)

            def copy_v(b, t):
                dve.wait_ge(proj_act, UNITS * b + 2 + t + 1)
                v = psP[:, t % 2, 0:NKV].rearrange("p (g d) -> p g d", g=G)
                dve.tensor_copy(v_pad[:, t, 4:8, HD:2 * HD], v[:, 4:8]).then_inc(proj_dve, 1)

            def copy_q(b, g):
                dve.wait_ge(proj_act, UNITS * b + 4 + g + 1)
                for h in range(HG):
                    ins = dve.tensor_tensor(q_stack[32:64, g % 4, h], psP[32 * h:32 * h + 32, g % 2, 0:T],
                                            f(q_stack[0:32, g % 4, h]), ALU.subtract)
                ins.then_inc(proj_dve, 1)

            def maxima(b, g):
                for n in range(TILES):
                    qt, hp = n // 2, n % 2
                    dve.wait_ge(s_done, TILES * (G * b + g) + n + 1)
                    dve.tensor_reduce(nmax[:, g % 2, 2 * hp:2 * hp + 2, qt],
                                      psS[:, n % 2].rearrange("p (h k) -> p h k", h=2),
                                      AX.X, ALU.max, negate=True).then_inc(s_max, 1)
                flat = nmax[:, g % 2].rearrange("p h q -> p (h q)")
                dve.wait_ge(s_max, TILES * (G * b + g + 1) + 2)
                dve.tensor_copy(nmax_parts[:, g % 2, 0:8], flat).then_inc(nmax_hi, 1)
                dve.wait_ge(nmax_hi, G * b + g + 1)
                dve.tensor_tensor(nmax_parts[:, g % 2, 8:16], flat, f(nmax_parts[:, g % 2, 0:8]),
                                  ALU.subtract).then_inc(nmax_lo, 1)

            def copy_o(b, g):
                dve.wait_ge(pv_done, 2 * (G * b + g) + 2)
                if g == 0:
                    dve.wait_ge(o_stored, 48 * b + 48)
                for hp in range(2):
                    dve.tensor_copy(o_sb[64 * hp:64 * hp + 64, g], psO[0:64, hp])
                dve.tensor_copy(den_sb[64:128, g], psO[64:128]).then_inc(o_copied, 1)

            def batch(b, last):
                for s in range(STEPS):
                    if 1 <= s <= G:
                        maxima(b, s - 1)
                    if s < G:
                        copy_q(b, s)
                    if s == G and not last:
                        split_h(b + 1)
                    if s == STEPS - 1 and not last:
                        for j in range(2):
                            copy_k(b + 1, j)
                    if s >= 3:
                        copy_o(b, s - 3)
                if not last:
                    dve.wait_ge(pv_done, 2 * G * b + 2 * G)
                    for t in range(2):
                        copy_v(b + 1, t)

            split_h(0)
            for j in range(2):
                copy_k(0, j)
            dve.wait_ge(filled, 3)
            for t in range(2):
                copy_v(0, t)
            with dve.Fori(0, B - 1) as b:
                batch(b, False)
            batch(B - 1, True)

        @block.tensor
        def _(pe):
            def project(b, unit, part):
                if part == 0 and unit >= 2:
                    pe.wait_ge(proj_act, UNITS * b + unit - 1)
                    pe.wait_ge(proj_dve, UNITS * b + unit - 1)
                out = psP[:, unit % 2, 0:T]
                for k in range(4 * part, 4 * part + 4):
                    for i, (w, h) in enumerate(((w_hi, h_hi), (w_hi, h_lo), (w_lo, h_hi))):
                        first, end = k == 0 and i == 0, k == KT - 1 and i == 2
                        if unit < 2:
                            c = D + unit * P
                            mm = pe.matmul(out, w[:, k, c:c + P], h[:, k], start=first, stop=end)
                        elif unit < 4:
                            t = (unit - 2) * P
                            mm = pe.matmul(out, h[:, k, t:t + P], w[:, k, D + NKV:NQKV], start=first, stop=end)
                        else:
                            c = (unit - 4) * P
                            mm = pe.matmul(out, w[:, k, c:c + P], h[:, k], start=first, stop=end)
                if part == 1:
                    mm.then_inc(proj_done, 1)

            def scores(b, g, n):
                if n == 0:
                    pe.wait_ge(proj_act, UNITS * b + 4 + g + 1)
                    pe.wait_ge(proj_dve, UNITS * b + 4 + g + 1)
                pe.wait_ge(s_max, TILES * (G * b + g) + n + 1)
                qt, hp = n // 2, n % 2
                for i in range(2):
                    mm = pe.matmul(psS[:, n % 2, i * T:(i + 1) * T],
                                   q_stack[0:96, g % 4, 2 * hp + i, qt * P:(qt + 1) * P], k_stack[0:96, g],
                                   start=True, stop=True)
                mm.then_inc(s_done, 1)

            def scores_t(b, g, n):
                if n == 0:
                    pe.wait_ge(rows_landed, 32 * (G * b + g) + 32)
                pe.wait_ge(exp_done, TILES * (G * b + g) + n + 1)
                hp, kt = n // 2, n % 2
                pe.matmul(psT[:, n % 2], k_stack[0:98, g, kt * P:(kt + 1) * P],
                          q_stack[0:98, g % 4, 2 * hp:2 * hp + 2].rearrange("p h t -> p (h t)"),
                          start=True, stop=True).then_inc(st_done, 1)

            def outputs(b, g, hp):
                if hp == 0:
                    pe.wait_ge(exp_done, TILES * (G * b + g + 1) + 2)
                    pe.wait_ge(o_copied, G * b + g + 1)
                for i in range(2):
                    c = HD * (1 - i)
                    for kt in range(KK):
                        mm = pe.matmul(psO[:, hp], v_pad[:, kt, g, c:c + P],
                                       probs[:, g % 2, kt, (2 * hp + i) * T:(2 * hp + i + 1) * T],
                                       start=(i == 0 and kt == 0), stop=(i == 1 and kt == 1))
                mm.then_inc(pv_done, 1)

            def turn(b, g):
                pe.wait_ge(nmax_lo, G * b + g + 1)
                pe.transpose(psM[0:16, 0:P], f(nmax_parts[:, g % 2]), id_sb[:]).then_inc(turned, 1)

            def batch(b, last):
                for s in range(STEPS):
                    if s < G:
                        project(b, 4 + s, 0)
                    if 1 <= s <= G:
                        scores(b, s - 1, 0)
                        scores(b, s - 1, 1)
                    if s < G:
                        project(b, 4 + s, 1)
                    if 1 <= s <= G:
                        scores(b, s - 1, 2)
                        scores(b, s - 1, 3)
                    for hp in range(2):
                        if 2 <= s < G + 2:
                            scores_t(b, s - 2, 2 * hp)
                            scores_t(b, s - 2, 2 * hp + 1)
                        if s >= 3:
                            outputs(b, s - 3, hp)
                    if 1 <= s <= G:
                        turn(b, s - 1)
                    if s == G and not last:
                        pe.wait_ge(h_lo_done, b + 2)
                        for unit in range(2):
                            project(b + 1, unit, 0)
                            project(b + 1, unit, 1)
                    if s >= G + 1 and not last:
                        project(b + 1, 2 + s - G - 1, 0)
                        project(b + 1, 2 + s - G - 1, 1)

            pe.wait_ge(w_lo_done, KT)
            pe.wait_ge(h_lo_done, 1)
            pe.wait_ge(id_landed, 16)
            for unit in range(4):
                project(0, unit, 0)
                project(0, unit, 1)
            pe.wait_ge(filled, 3)
            with pe.Fori(0, B - 1) as b:
                batch(b, False)
            batch(B - 1, True)


def finish(nc, xT, oT, den, rden, Wo, idx, cond2, RA, ffn_B, ident, outT):
    ROWS = 4
    with ExitStack() as ctx:
        def sb(name, shape, dt=F32):
            return ctx.enter_context(nc.sbuf_tensor(name, shape, dt))

        def psum(name, shape):
            return ctx.enter_context(nc.psum_tensor(name, shape, F32))

        def sem(name):
            return ctx.enter_context(nc.semaphore(name))

        id_sb = sb("id_sb3", [P, P])
        idx_sb = sb("idx_sb3", [1, B], I32)
        ra_sb = sb("ra_sb", [P, KT, EC])
        fb_sb = sb("fb_sb", [ER, D])
        wo_raw = sb("wo_raw", [P, 2, D])
        wo_hi, wo_lo = sb("wo_hi", [P, KT, D], F32R), sb("wo_lo", [P, KT, D], F32R)
        o_raw = sb("o_raw", [P, 2, G, T])
        o_scale = sb("o_scale", [P, 2, G, T])
        den_sb = sb("den_sb3", [P, 2, 64])
        rden_sb = sb("rden_sb3", [P, 2, 64])
        o_hi, o_lo = sb("o_hi", [P, 2, G, T], F32R), sb("o_lo", [P, 2, G, T], F32R)
        x_sb = sb("x_sb", [P, 2, KT, T])
        cond = sb("cond", [P, ROWS, D])
        g_sb = sb("g_sb", [EC, D])
        g_t = sb("g_t", [P, KT, EC])
        mid = sb("mid", [P, 2, EC])
        rank0 = sb("rank0", [P, 2, E])
        rank = sb("rank", [P, 2, E])
        beats = sb("beats", [P, 2, E])
        top = sb("top", [P, 2])
        gate = sb("gate", [P, 2, E])
        gsum = sb("gsum", [P, 2])
        gated = sb("gated", [P, 2, EC])
        gated_t = sb("gated_t", [ER, T])

        psW = psum("psW", [P, 2, 512])
        psG = psum("psG", [P, 2, 512])
        psX = psum("psX", [P, 512])
        psY = psum("psY", [P, 2, 512])

        const_landed = sem("const_landed")
        wo_landed = [sem(f"wo_landed{i}") for i in range(2)]
        wo_hi_done, wo_lo_done = sem("wo_hi_done"), sem("wo_lo_done")
        den_landed, rden_done, rden_stored = sem("den_landed"), sem("rden_done"), sem("rden_stored")
        in_landed, x_landed = sem("o_landed"), sem("x_landed")
        o_scaled, o_hi_done, o_lo_done = sem("o_scaled"), sem("o_hi_done"), sem("o_lo_done")
        wo_done, x2_done = sem("wo_done"), sem("x2_done")
        cond_landed = [sem(f"cond_landed{i}") for i in range(ROWS)]
        cond_used = sem("cond_used")
        g_copied = sem("g_copied")
        gt_done, gt_copied = sem("gt_done"), sem("gt_copied")
        mid_done, mid_copied = sem("mid_done"), sem("mid_copied")
        chain = sem("chain")
        shifted, exp_done = sem("shifted"), sem("gate_exp_done")
        gated_done, turned, turned_copied = sem("gated_done"), sem("gated_turned"), sem("turned_copied")
        y_done, y_added = sem("y_done"), sem("y_added")
        stored = sem("stored")
        block = ctx.enter_context(nc.Block())

        @block.sync
        def _(sp):
            for dst, src in ((id_sb[:], ident), (idx_sb[:], idx), (ra_sb[:], RA), (fb_sb[:], ffn_B)):
                sp.dma_start(dst, src).then_inc(const_landed, 16)
            for k in range(KT):
                if k >= 2:
                    sp.wait_ge(wo_lo_done, k - 1)
                sp.dma_start(wo_raw[:, k % 2], Wo[k * P:(k + 1) * P]).then_inc(wo_landed[k % 2], 16)

            def load_o(pair):
                two = bass.ds(2 * pair, 2)
                sp.dma_start(den_sb[:], den[two].rearrange("b c g h t -> b (c g h t)")
                             .rearrange("b (p n) -> p b n", p=P)).then_inc(den_landed, 16)
                sp.dma_start(o_raw[:], oT[two].rearrange("b p g t -> p b (g t)")).then_inc(in_landed, 16)
                sp.wait_ge(rden_done, pair + 1)
                sp.dma_start(rden[two].rearrange("b c g h t -> b (c g h t)")
                             .rearrange("b (p n) -> p b n", p=P), rden_sb[:]).then_inc(rden_stored, 16)
                sp.wait_ge(rden_stored, 16 * pair + 16)
                for h in range(HG):
                    for c in range(2):
                        src = rden[bass.ds(2 * pair + c, 1), h % 2, :, h // 2].to_broadcast([32, G, T])
                        sp.dma_start(o_scale[32 * h:32 * h + 32, c], src).then_inc(in_landed, 16)

            def load_x(pair):
                sp.dma_start(x_sb[:], xT[bass.ds(2 * pair, 2)].rearrange("b p k t -> p b (k t)")
                             ).then_inc(x_landed, 16)

            def store(pair):
                sp.wait_ge(y_added, 2 * KT * pair + 2 * KT + 2)
                sp.dma_start(outT[bass.ds(2 * pair, 2)].rearrange("b p k t -> p b (k t)"), x_sb[:]
                             ).then_inc(stored, 16)
                sp.wait_ge(stored, 16 * pair + 16)

            load_o(0)
            load_x(0)
            with sp.Fori(0, PAIRS - 1) as pair:
                sp.wait_ge(o_lo_done, pair + 1)
                load_o(pair + 1)
                store(pair)
                load_x(pair + 1)
            store(PAIRS - 1)

        @block.gpsimd
        def _(pool):
            pool.wait_ge(const_landed, 64)
            for s in range(ROWS):
                slot = pool.value_load(idx_sb[0:1, 0:1], min_val=0, max_val=7)
                pool.dma_start(cond[:, s], cond2[bass.ds(slot, 1), s].rearrange("s p d -> (s p) d")
                               ).then_inc(cond_landed[s], 16)

            def rows(n):
                slot = pool.value_load(idx_sb[0:1, bass.ds(n, 1)], min_val=0, max_val=7)
                for k in range(ROWS, KT):
                    pool.wait_ge(cond_used, KT * n + k - ROWS + 1)
                    pool.dma_start(cond[:, k % ROWS], cond2[bass.ds(slot, 1), k].rearrange("s p d -> (s p) d")
                                   ).then_inc(cond_landed[k % ROWS], 16)

            def next_rows(n):
                slot = pool.value_load(idx_sb[0:1, bass.ds(n + 1, 1)], min_val=0, max_val=7)
                for k in range(ROWS):
                    pool.wait_ge(cond_used, KT * n + KT - ROWS + k + 1)
                    pool.dma_start(cond[:, k], cond2[bass.ds(slot, 1), k].rearrange("s p d -> (s p) d")
                                   ).then_inc(cond_landed[k], 16)

            with pool.Fori(0, PAIRS - 1) as pair:
                rows(2 * pair)
                next_rows(2 * pair)
                rows(2 * pair + 1)
                next_rows(2 * pair + 1)
            rows(B - 2)
            next_rows(B - 2)
            rows(B - 1)

        @block.scalar
        def _(act):
            act.sem_inc(g_copied, 1)
            for k in range(KT):
                act.wait_ge(wo_landed[k % 2], 16 * (k // 2 + 1))
                nc.scalar.activation(wo_hi[:, k], wo_raw[:, k % 2], ACT.Copy).then_inc(wo_hi_done, 1)

            def split_o(pair):
                act.wait_ge(o_scaled, pair + 1)
                nc.scalar.activation(o_hi[:], o_raw[:], ACT.Copy).then_inc(o_hi_done, 1)

            def batch(n):
                act.wait_ge(cond_used, KT * (n + 1))
                nc.scalar.activation(g_sb[:], psG[0:EC].rearrange("p a b -> p (a b)"), ACT.Copy).then_inc(g_copied, 1)
                act.wait_ge(shifted, n + 1)
                nc.scalar.activation(gate[:], beats[:], ACT.Exp).then_inc(exp_done, 1)
                act.wait_ge(turned, n + 1)
                nc.scalar.activation(gated_t[:], psX[0:ER, 0:T], ACT.Copy, scale=FFN_SCALE).then_inc(turned_copied, 1)

            split_o(0)
            with act.Fori(0, PAIRS - 1) as pair:
                for c in range(2):
                    batch(2 * pair + c)
                split_o(pair + 1)
            for c in range(2):
                batch(B - 2 + c)

        @block.vector
        def _(dve):
            dve.sem_inc(x2_done, 2)
            dve.sem_inc(y_added, 2)
            dve.memset(gated[:, :, ER:EC], 0.0)
            for e in range(E):
                ins = dve.memset(rank0[:, :, e:e + 1], float(e))
            ins.then_inc(chain, 1)
            for k in range(KT):
                dve.wait_ge(wo_hi_done, k + 1)
                dve.tensor_tensor(wo_lo[:, k], wo_raw[:, k % 2], f(wo_hi[:, k]), ALU.subtract).then_inc(wo_lo_done, 1)

            def split_o(pair):
                dve.wait_ge(den_landed, 16 * pair + 16)
                dve.reciprocal(rden_sb[:], den_sb[:]).then_inc(rden_done, 1)
                dve.wait_ge(in_landed, 16 * 9 * (pair + 1))
                dve.tensor_tensor(o_raw[:], o_raw[:], o_scale[:], ALU.mult).then_inc(o_scaled, 1)
                dve.wait_ge(o_hi_done, pair + 1)
                dve.tensor_tensor(o_lo[:], o_raw[:], f(o_hi[:]), ALU.subtract).then_inc(o_lo_done, 1)

            def residual(pair):
                dve.wait_ge(x_landed, 16 * pair + 16)
                for m in range(KT):
                    dve.wait_ge(wo_done, KT * pair + m + 1)
                    dve.tensor_tensor(x_sb[:, :, m], x_sb[:, :, m],
                                      psW[:, m % 2].rearrange("p (b t) -> p b t", b=2), ALU.add).then_inc(x2_done, 1)

            CH = 15

            def batch(n):
                done = [0]

                def step(ins):
                    done[0] += 1
                    ins.then_inc(chain, 1)
                    dve.wait_ge(chain, CH * n + done[0] + 1)

                dve.wait_ge(gt_done, 2 * n + 1)
                dve.tensor_copy(g_t[:, 0:4], psX[:, 0:4 * EC].rearrange("p (k e) -> p k e", k=4)).then_inc(gt_copied, 1)
                dve.wait_ge(gt_done, 2 * n + 2)
                dve.tensor_copy(g_t[:, 4:8], psX[:, 0:4 * EC].rearrange("p (k e) -> p k e", k=4)).then_inc(gt_copied, 1)
                dve.wait_ge(mid_done, n + 1)
                step(dve.tensor_copy(mid[:], psX[:, 0:2 * EC].rearrange("p (t e) -> p t e", t=2)))
                logit = mid[:, :, ER:EC]
                for d in range(1, E):
                    step(dve.tensor_tensor(beats[:, :, 0:E - d], logit[:, :, d:E], logit[:, :, 0:E - d], ALU.is_gt))
                    if d == 1:
                        step(dve.tensor_copy(rank[:], rank0[:]))
                    step(dve.tensor_tensor(rank[:, :, 0:E - d], rank[:, :, 0:E - d], beats[:, :, 0:E - d], ALU.add))
                    step(dve.tensor_tensor(rank[:, :, d:E], rank[:, :, d:E], beats[:, :, 0:E - d], ALU.subtract))
                step(dve.tensor_reduce(top[:], logit, AX.X, ALU.max))
                for t in range(2):
                    ins = dve.tensor_scalar(beats[:, t], logit[:, t], top[:, t:t + 1], None, ALU.subtract)
                ins.then_inc(shifted, 1)
                dve.wait_ge(exp_done, n + 1)
                step(dve.scalar_tensor_tensor(gate[:], rank[:], 1.5, gate[:], ALU.is_lt, ALU.mult))
                step(dve.tensor_reduce(gsum[:], gate[:], AX.X, ALU.add))
                dve.reciprocal(gsum[:], gsum[:]).then_inc(chain, 1)
                dve.wait_ge(chain, CH * n + CH + 1)
                for t in range(2):
                    for e in range(E):
                        ins = dve.tensor_scalar(gated[:, t, e * R:(e + 1) * R], mid[:, t, e * R:(e + 1) * R],
                                                gate[:, t, e:e + 1], gsum[:, t:t + 1], ALU.mult, ALU.mult)
                ins.then_inc(gated_done, 1)
                assert done[0] + 1 == CH
                for m in range(KT):
                    dve.wait_ge(y_done, KT * n + m + 1)
                    c = n_parity[0]
                    dve.tensor_tensor(x_sb[:, c, m], x_sb[:, c, m], psY[:, m % 2, 0:T], ALU.add).then_inc(y_added, 1)

            n_parity = [0]
            split_o(0)
            with dve.Fori(0, PAIRS - 1) as pair:
                residual(pair)
                for c in range(2):
                    n_parity[0] = c
                    batch(2 * pair + c)
                split_o(pair + 1)
            residual(PAIRS - 1)
            for c in range(2):
                n_parity[0] = c
                batch(B - 2 + c)

        @block.tensor
        def _(pe):
            pe.wait_ge(wo_lo_done, KT)
            pe.wait_ge(const_landed, 64)
            with pe.Fori(0, PAIRS) as pair:
                pe.wait_ge(o_lo_done, pair + 1)
                for m in range(KT):
                    pe.wait_ge(x2_done, KT * pair + m + 1)
                    cols = slice(m * P, (m + 1) * P)
                    n = 0
                    for k in range(KT):
                        for w, o in ((wo_hi, o_hi), (wo_hi, o_lo), (wo_lo, o_hi)):
                            mm = pe.matmul(psW[:, m % 2].rearrange("p (b t) -> p b t", b=2), w[:, k, cols],
                                           o[:, :, k], start=(n == 0), stop=(n == 3 * KT - 1))
                            n += 1
                    mm.then_inc(wo_done, 1)
                for c in range(2):
                    nb = 2 * pair + c
                    pe.wait_ge(g_copied, nb + 1)
                    for k in range(KT):
                        pe.wait_ge(cond_landed[k % ROWS], 16 * (2 * nb + k // ROWS + 1))
                        for half in range(2):
                            mm = pe.matmul(psG[0:EC, half], ra_sb[:, k], cond[:, k % ROWS, half * 512:(half + 1) * 512],
                                           start=(k == 0), stop=(k == KT - 1))
                        mm.then_inc(cond_used, 1)
                    pe.wait_ge(g_copied, nb + 2)
                    for half in range(2):
                        if half == 1:
                            pe.wait_ge(gt_copied, 2 * nb + 1)
                        for k in range(4):
                            kk = 4 * half + k
                            mm = pe.transpose(psX[:, k * EC:(k + 1) * EC], g_sb[:, kk * P:(kk + 1) * P],
                                              id_sb[0:EC, 0:EC])
                        mm.then_inc(gt_done, 1)
                    pe.wait_ge(x2_done, KT * pair + KT + 2)
                    pe.wait_ge(gt_copied, 2 * nb + 2)
                    for t in range(2):
                        for k in range(KT):
                            mm = pe.matmul(psX[:, t * EC:(t + 1) * EC], x_sb[:, c, k, t * P:(t + 1) * P], g_t[:, k],
                                           start=(k == 0), stop=(k == KT - 1))
                    mm.then_inc(mid_done, 1)
                    pe.wait_ge(gated_done, nb + 1)
                    for t in range(2):
                        mm = pe.transpose(psX[0:EC, t * P:(t + 1) * P], gated[:, t], id_sb[:])
                    mm.then_inc(turned, 1)
                    pe.wait_ge(turned_copied, nb + 1)
                    for m in range(KT):
                        pe.wait_ge(y_added, KT * nb + m + 1)
                        pe.matmul(psY[:, m % 2, 0:T], fb_sb[:, m * P:(m + 1) * P], gated_t[:],
                                  start=True, stop=True).then_inc(y_done, 1)


_INS = ["xT", "itok_A", "itok_C", "WT", "bias", "lora_A", "lora_B", "Wqkv", "Wo", "cond2", "RA", "ffn_B", "ident"]


def build(nc, a, outT):
    hT = nc.dram_tensor("h_scratch", (B, P, KT, T), F32).ap()
    oT = nc.dram_tensor("o_scratch", (B, P, G, T), F32).ap()
    den = nc.dram_tensor("den_scratch", (B, 2, G, 2, T), F32).ap()
    rden = nc.dram_tensor("rden_scratch", (B, 2, G, 2, T), F32).ap()
    project_tokens(nc, a["xT"], a["itok_A"], a["WT"], a["bias"], a["lora_A"], a["lora_B"], hT)
    attend(nc, hT, a["Wqkv"], a["ident"], oT, den)
    finish(nc, a["xT"], oT, den, rden, a["Wo"], a["itok_C"], a["cond2"], a["RA"], a["ffn_B"], a["ident"], outT)


def kernel(x, itok_B_0_23, itok_B_3_7, L0_cond_W, L0_cond_b, L0_cond_lora_As, L0_cond_lora_Bs, L0_attn_w_q,
           L0_attn_w_k, L0_attn_w_v, L0_attn_w_o, L0_cond2_weight, L0_ffn_router_w, L0_ffn_A, L0_ffn_B):
    import concourse.bacc as _bacc
    from concourse.bass_utils import run_bass_kernel_spmd as _run

    def tiles(a):
        a = a.reshape(a.shape[:-2] + (KT, P, a.shape[-1]))
        return np.swapaxes(a, -3, -2)

    x = np.asarray(x)
    arrays = {
        "xT": tiles(np.swapaxes(x, 1, 2)),
        "itok_A": np.asarray(itok_B_0_23).reshape(1, B),
        "itok_C": np.asarray(itok_B_3_7).reshape(1, B),
        "WT": tiles(np.asarray(L0_cond_W).T),
        "bias": np.asarray(L0_cond_b).reshape(KT, P).T,
        "lora_A": tiles(np.asarray(L0_cond_lora_As)),
        "lora_B": np.asarray(L0_cond_lora_Bs),
        "Wqkv": np.concatenate([np.asarray(w) for w in (L0_attn_w_q, L0_attn_w_k, L0_attn_w_v)], axis=1),
        "Wo": np.asarray(L0_attn_w_o),
        "cond2": np.asarray(L0_cond2_weight).reshape(-1, KT, P, D),
        "RA": tiles(np.concatenate([np.asarray(L0_ffn_A).reshape(ER, D), np.asarray(L0_ffn_router_w)], axis=0).T),
        "ffn_B": np.swapaxes(np.asarray(L0_ffn_B), 1, 2).reshape(ER, D),
        "ident": np.eye(P, dtype=np.float32),
    }
    nc = _bacc.Bacc("TRN2", target_bir_lowering=False, num_devices=1)
    aps, sent = {}, {}
    for name in _INS:
        v = np.ascontiguousarray(arrays[name])
        sent[f"in_{name}"] = v
        aps[name] = nc.dram_tensor(f"in_{name}", v.shape, mybir.dt.from_np(v.dtype), kind="ExternalInput").ap()
    outT = nc.dram_tensor("outT", (B, P, KT, T), F32, kind="ExternalOutput").ap()
    build(nc, aps, outT)
    r = _run(nc, [sent], core_ids=[0])
    out = r.results[0]["outT"]
    return np.ascontiguousarray(out.transpose(0, 3, 2, 1).reshape(B, T, D))
```

```python
from contextlib import ExitStack

import numpy as np

import concourse.bass as bass
from concourse import mybir

P = 128
B, T, D = 8, 256, 1024
KT = D // P
H, G, HD = 32, 8, 32
HG = H // G
NKV = G * HD
NQKV = D + 2 * NKV
R = 16
LORA_SCALE = 2.0
E = 4
ER = E * R
EC = ER + E
FFN_SCALE = 4.0
T2 = 2 * T
PAIRS = B // 2
ATT_SCALE = float(HD) ** -0.5

F32 = mybir.dt.float32
F32R = mybir.dt.float32r
I32 = mybir.dt.int32
ACT = mybir.ActivationFunctionType
ALU = mybir.AluOpType
AX = mybir.AxisListType

RING = 3
W_TILES = KT
QKV_TILES = NQKV // P
WO_TILES = KT


def f(ap):
    return ap.bitcast(F32)


class Weights:

    def __init__(self, nc, sb, sem):
        self.nc = nc
        self.raw = sb("weight_raw", [P, RING, D])
        self.landed = [sem(f"weight_landed{i}") for i in range(RING)]
        self.hi_done = sem("weight_hi_done")
        self.lo_done = sem("weight_lo_done")

    def load(self, eng, n, src):
        if n >= RING:
            eng.wait_ge(self.lo_done, n - RING + 1)
        dst = self.raw[:, n % RING]
        if len(src.shape) == 3:
            dst = dst.rearrange("p (k c) -> p k c", c=src.shape[2])
        eng.dma_start(dst, src).then_inc(self.landed[n % RING], 16)

    def split_hi(self, act, n, hi):
        act.wait_ge(self.landed[n % RING], 16 * (n // RING + 1))
        self.nc.scalar.activation(hi, self.raw[:, n % RING], ACT.Copy).then_inc(self.hi_done, 1)

    def split_lo(self, dve, n, hi, lo):
        dve.wait_ge(self.hi_done, n + 1)
        dve.tensor_tensor(lo, self.raw[:, n % RING], f(hi), ALU.subtract).then_inc(self.lo_done, 1)


class Stage:
    pass


def tokens_stage(nc, sem, weights, wq, load_qkv, xT, idx, WT, bias, lora_A, lora_B, hT):
    SLOTS = 4
    BANK = [0, 1, 2, 3, 4, 5, 6, 3]
    AB_DMAS = 8
    st = Stage()
    with ExitStack() as ctx:
        def sb(name, shape, dt=F32):
            return ctx.enter_context(nc.sbuf_tensor(name, shape, dt))

        sb("qkv_head", [P, 4, 2, D])
        x_hi, x_lo = sb("x_hi", [P, KT, T2], F32R), sb("x_lo", [P, KT, T2], F32R)
        x_raw = sb("x_raw", [P, KT, T2])
        w_hi, w_lo = sb("w_hi", [P, KT, D], F32R), sb("w_lo", [P, KT, D], F32R)
        idx_sb = sb("idx_sb", [1, B], I32)
        bias_sb = sb("bias_sb", [P, KT])
        a_raw = sb("a_raw", [P, 2, KT, R])
        a_hi, a_lo = sb("a_hi", [P, 2, KT, R], F32R), sb("a_lo", [P, 2, KT, R], F32R)
        b_raw = sb("b_raw", [96, 2, D])
        b_stack = sb("b_stack", [96, 2, D], F32R)
        u_stack = sb("u_stack", [96, 2, T], F32R)
        h_out = sb("h_out", [P, SLOTS, T2])
        psH = ctx.enter_context(nc.psum_tensor("psH", [P, 7, T2], F32))
        psU = ctx.enter_context(nc.psum_tensor("psU", [P, T2], F32))

        idx_landed, bias_landed = sem("idx_landed"), sem("bias_landed")
        x_landed = [sem(f"x_landed{k}") for k in range(KT)]
        ab_landed = sem("ab_landed")
        zeroed = sem("zeroed")
        x_hi_done, x_lo_done, x_used = sem("x_hi_done"), sem("x_lo_done"), sem("x_used")
        ab_hi_done, ab_lo_done = sem("ab_hi_done"), sem("ab_lo_done")
        u_done, u_hi_done, u_lo_done = sem("u_done"), sem("u_hi_done"), sem("u_lo_done")
        h_done, h_copied = sem("h_done"), sem("h_copied")
        h_stored = [sem(f"h_stored{i}") for i in range(SLOTS)]
        st.h_done, st.h_copied, st.h_stored, st.idx = h_done, h_copied, h_stored, idx_sb
        st.h_all = 16 * PAIRS * KT // SLOTS
        st.tiles = PAIRS * KT

    def both(ap):
        return ap.rearrange("p (b t) -> p b t", b=2)

    def sync(sp):
        def load_x(pair, k):
            sp.dma_start(both(x_raw[:, k]), xT[bass.ds(2 * pair, 2), :, k].rearrange("b p t -> p b t")
                         ).then_inc(x_landed[k], 16)

        def load_ab(pair):
            for c in range(2):
                slot = sp.value_load(idx_sb[0:1, bass.ds(2 * pair + c, 1)], min_val=0, max_val=31)
                sp.dma_start(a_raw[:, c], lora_A[bass.ds(slot, 1)].rearrange("s p k r -> p (s k) r")
                             ).then_inc(ab_landed, 16)
                for q in range(3):
                    sp.dma_start(b_raw[32 * q:32 * q + R, c], lora_B[bass.ds(slot, 1)].rearrange("s r d -> (s r) d")
                                 ).then_inc(ab_landed, 16)

        def pair_program(pair, last):
            if not last:
                for k in range(KT):
                    sp.wait_ge(x_lo_done, KT * pair + k + 1)
                    load_x(pair + 1, k)
                sp.wait_ge(ab_lo_done, pair + 1)
                load_ab(pair + 1)
            for s in range(KT):
                dst = hT[bass.ds(2 * pair, 2), :, s].rearrange("b p t -> p b t")
                sp.wait_ge(h_copied, KT * pair + s + 1)
                sp.dma_start(dst, both(h_out[:, s % SLOTS])).then_inc(h_stored[s % SLOTS], 16)

        sp.dma_start(idx_sb[:], idx).then_inc(idx_landed, 16)
        for k in range(KT):
            load_x(0, k)
        sp.dma_start(bias_sb[:], bias).then_inc(bias_landed, 16)
        sp.wait_ge(idx_landed, 16)
        sp.wait_ge(zeroed, 1)
        load_ab(0)
        with sp.Fori(0, PAIRS - 1) as pair:
            pair_program(pair, False)
        pair_program(PAIRS - 1, True)

    def gpsimd(pool):
        for k in range(W_TILES):
            weights.load(pool, k, WT[:, k])
        for i in range(7):
            load_qkv(pool, i)

    def scalar(act):
        def split_x(pair, k):
            act.wait_ge(x_landed[k], 16 * pair + 16)
            if not isinstance(pair, int) or pair > 0:
                act.wait_ge(x_used, KT * (pair - 1) + k + 1)
            nc.scalar.activation(x_hi[:, k], x_raw[:, k], ACT.Copy).then_inc(x_hi_done, 1)

        def pair_program(pair, first, last):
            act.wait_ge(ab_landed, 16 * AB_DMAS * (pair + 1))
            nc.scalar.activation(a_hi[:], a_raw[:], ACT.Copy)
            nc.scalar.activation(b_stack[:], b_raw[:], ACT.Copy).then_inc(ab_hi_done, 1)
            act.wait_ge(u_done, pair + 1)
            for q in (0, 1):
                nc.scalar.activation(u_stack[32 * q:32 * q + R], both(psU[0:R]), ACT.Copy,
                                     scale=LORA_SCALE).then_inc(u_hi_done, 1)
            for s in range(KT):
                if s == 4:
                    if last:
                        for i in range(4):
                            weights.split_hi(act, W_TILES + i, wq[:, i, 0])
                    else:
                        for k in range(KT):
                            split_x(pair + 1, k)
                act.wait_ge(h_done, KT * pair + s + 1)
                if s >= SLOTS or not first:
                    act.wait_ge(h_stored[s % SLOTS], 16 * (KT // SLOTS * pair + s // SLOTS))
                nc.scalar.activation(h_out[:, s % SLOTS], psH[:, BANK[s]], ACT.Identity,
                                     bias=bias_sb[:, s:s + 1]).then_inc(h_copied, 1)

        for k in range(KT):
            split_x(0, k)
            weights.split_hi(act, k, w_hi[:, k])
        act.wait_ge(bias_landed, 16)
        act.wait_ge(zeroed, 2)
        pair_program(0, True, False)
        with act.Fori(1, PAIRS - 1) as pair:
            pair_program(pair, False, False)
        pair_program(PAIRS - 1, False, True)

    def vector(dve):
        def split_x(pair, k):
            dve.wait_ge(x_hi_done, KT * pair + k + 1)
            dve.tensor_tensor(x_lo[:, k], x_raw[:, k], f(x_hi[:, k]), ALU.subtract).then_inc(x_lo_done, 1)

        def pair_program(pair, last):
            dve.wait_ge(ab_hi_done, pair + 1)
            dve.tensor_tensor(b_stack[32:64], b_raw[32:64], f(b_stack[32:64]), ALU.subtract)
            dve.tensor_tensor(a_lo[:], a_raw[:], f(a_hi[:]), ALU.subtract).then_inc(ab_lo_done, 1)
            dve.wait_ge(u_hi_done, 2 * pair + 2)
            dve.scalar_tensor_tensor(u_stack[64:64 + R], both(psU[0:R]), LORA_SCALE, f(u_stack[0:R]),
                                     ALU.mult, ALU.subtract).then_inc(u_lo_done, 1)
            if last:
                for i in range(4):
                    weights.split_lo(dve, W_TILES + i, wq[:, i, 0], wq[:, i, 1])
            else:
                for k in range(KT):
                    split_x(pair + 1, k)

        dve.memset(b_raw[:], 0.0).then_inc(zeroed, 1)
        dve.memset(f(u_stack[:]), 0.0).then_inc(zeroed, 1)
        for k in range(KT):
            split_x(0, k)
            weights.split_lo(dve, k, w_hi[:, k], w_lo[:, k])
        with dve.Fori(0, PAIRS - 1) as pair:
            pair_program(pair, False)
        pair_program(PAIRS - 1, True)

    def tensor(pe):
        def products(m, k, first):
            cols = slice(m * P, (m + 1) * P)
            for i, (w, x) in enumerate(((w_hi, x_hi), (w_hi, x_lo), (w_lo, x_hi))):
                mm = pe.matmul(psH[:, BANK[m]], w[:, k, cols], x[:, k], start=(first and i == 0), stop=False)
            return mm

        def low_rank(m):
            for c in range(2):
                mm = pe.matmul(psH[:, BANK[m], c * T:(c + 1) * T], b_stack[:, c, m * P:(m + 1) * P],
                               u_stack[:, c], start=False, stop=(c == 1))
            mm.then_inc(h_done, 1)

        def pair_program(pair, first):
            for k in range(KT):
                pe.wait_ge(x_lo_done, KT * pair + k + 1)
                if first:
                    pe.wait_ge(weights.lo_done, k + 1)
                if k == KT - 1:
                    pe.wait_ge(ab_lo_done, pair + 1)
                    for c in range(2):
                        n = 0
                        for kk in range(KT):
                            for a, x in ((a_hi, x_hi), (a_hi, x_lo), (a_lo, x_hi)):
                                mm = pe.matmul(psU[0:R, c * T:(c + 1) * T], a[:, c, kk],
                                               x[:, kk, c * T:(c + 1) * T], start=(n == 0), stop=(n == 3 * KT - 1))
                                n += 1
                    mm.then_inc(u_done, 1)
                for s in range(4):
                    if k == 0 and not first:
                        pe.wait_ge(h_copied, KT * pair if s == 3 else KT * (pair - 1) + s + 1)
                    products(s, k, k == 0)
            pe.wait_ge(u_lo_done, pair + 1)
            for s in range(4):
                low_rank(s)
            for k in range(KT):
                for s in range(4, KT):
                    if k == 0 and s == 7:
                        pe.wait_ge(h_copied, KT * pair + 4)
                    elif k == 0 and not first:
                        pe.wait_ge(h_copied, KT * (pair - 1) + s + 1)
                    mm = products(s, k, k == 0)
                mm.then_inc(x_used, 1)
            for s in range(4, KT):
                low_rank(s)

        pair_program(0, True)
        with pe.Fori(1, PAIRS) as pair:
            pair_program(pair, False)

    st.sync, st.gpsimd, st.scalar, st.vector, st.tensor = sync, gpsimd, scalar, vector, tensor
    return st


def attend_stage(nc, sem, weights, wq, act_raw, load_qkv, load_wo, before, ident, hT, oT, den):
    KK = 2
    N = B * G
    TILES = 4
    UNITS = ["k0", "q0", "q1", "q2", "v0", "v1", "q3", "k1", "q4", "q5", "q6", "q7"]
    NU = len(UNITS)
    SPLIT_AT = [[4, 5], [6, 7], [8], [9], [10], [11], [], []]
    st = Stage()
    with ExitStack() as ctx:
        def sb(name, shape, dt=F32):
            return ctx.enter_context(nc.sbuf_tensor(name, shape, dt))

        def psum(name, shape):
            return ctx.enter_context(nc.psum_tensor(name, shape, F32))

        sb("qkv_all", [P, QKV_TILES, 2, D])
        h_hi, h_lo = sb("h_hi", [P, KT, T], F32R), sb("h_lo", [P, KT, T], F32R)
        k_stack = sb("k_stack", [98, G, T], F32R)
        q_stack = sb("q_stack", [98, 4, HG, T], F32R)
        v_pad = sb("v_pad", [P, KK, G, 5 * HD])
        id_sb = sb("id_sb", [P, P])
        nmax = sb("nmax", [P, 2, HG, 2])
        nmax_parts = sb("nmax_parts", [P, 2, 2 * HG * 2], F32R)
        nmax_rows = sb("nmax_rows", [2 * HG * 2, 2, P])
        probs = sb("probs", [P, 2, KK, HG * T])
        o_sb = sb("o_sb", [P, 4, 2, T])

        psP = psum("psP", [P, 2, 512])
        psS = psum("psS", [P, 2, 512])
        psT = psum("psT", [P, 2, 512])
        psO = psum("psO", [P, 2, T])
        psM = psum("psM", [P, P])

        id_landed, filled = sem("id_landed"), sem("filled")
        h_landed, h_hi_done, h_lo_done = sem("h_landed"), sem("h_hi_done"), sem("h_lo_done")
        proj_done = sem("proj_done")
        proj_act, proj_dve = sem("proj_act"), sem("proj_dve")
        q_hi_done, q_ready = sem("q_hi_done"), sem("q_ready")
        s_done, s_max = sem("s_done"), sem("s_max")
        nmax_hi, nmax_lo = sem("nmax_hi"), sem("nmax_lo")
        turned, rows_done, rows_landed = sem("turned"), sem("rows_done"), sem("rows_landed")
        st_done, exp_done = sem("st_done"), sem("exp_done")
        pv_done, o_copied = sem("pv_done"), sem("o_copied")
        o_stored = [sem(f"o_stored{i}") for i in range(4)]
        st.proj_done, st.units, st.h_lo_done, st.h_splits = proj_done, NU * B, h_lo_done, 4 * B
        st.pv_done, st.o_copied, st.exp_done = pv_done, o_copied, exp_done
        st.o_stored, st.o_all, st.steps = o_stored, 32 * N // 4, N
        st.rows_landed = rows_landed

    def live(n):
        return not isinstance(n, int) or 0 <= n < N

    def at(b, unit):
        return NU * b + UNITS.index(unit) + 1

    def has_next(b):
        return not isinstance(b, int) or b < B - 1

    def run(eng, step, peel_last):
        for g in range(G):
            step(g, g, 0)
        with eng.Fori(1, B - 1 if peel_last else B) as b:
            for g in range(G):
                step(G * b + g, g, b)
        if peel_last:
            for g in range(G):
                step(G * (B - 1) + g, g, B - 1)
        for g in range(3):
            step(N + g, g, B)

    def sync(sp):
        def load_h(b):
            sp.dma_start(act_raw[:], hT[bass.ds(b, 1)].rearrange("b p k t -> p (b k t)")).then_inc(h_landed, 16)

        def step(n, g, b):
            if g == 1 and has_next(b):
                sp.wait_ge(h_lo_done, 4 * b + 4)
                load_h(b + 1)
            if live(n - 1):
                sp.wait_ge(rows_done, n)
                r = (g - 1) % 2
                for part in range(2):
                    sp.dma_start(f(q_stack[96 + part:97 + part, (g - 1) % 4].rearrange("p h t -> p (h t)")),
                                 nmax_rows[8 * part:8 * part + 8, r]).then_inc(rows_landed, 16)
            if live(n - 3):
                sp.wait_ge(o_copied, n - 2)
                go, slot = (g - 3) % G, (g - 3) % 4
                bo = b if g >= 3 else b - 1
                ob = oT[bass.ds(bo, 1), :, go].rearrange("b (c p) t -> p (b c) t", c=2)
                sp.dma_start(ob, o_sb[0:64, slot]).then_inc(o_stored[slot], 16)
                db = den[bass.ds(bo, 1), :, go].rearrange("b a c t -> (b a) (c t)")
                sp.dma_start(db, o_sb[64:128:32, slot].rearrange("p c t -> p (c t)")).then_inc(o_stored[slot], 16)

        for s in before.h_stored:
            sp.wait_ge(s, before.h_all)
        load_h(0)
        sp.wait_ge(before.h_done, before.tiles)
        sp.dma_start(id_sb[:], ident).then_inc(id_landed, 16)
        run(sp, step, True)

    def gpsimd(pool):
        pool.wait_ge(before.h_copied, before.tiles)
        for s in before.h_stored:
            pool.wait_ge(s, before.h_all)
        pool.memset(v_pad[:], 0.0).then_inc(filled, 1)
        pool.wait_ge(filled, 1)
        pool.memset(v_pad[:, :, :, 3 * HD:4 * HD], 1.0).then_inc(filled, 1)
        pool.wait_ge(filled, 2)
        pool.memset(f(k_stack[96:98]), 1.0).then_inc(filled, 1)
        for i in range(7, QKV_TILES):
            load_qkv(pool, i)
        for k in range(WO_TILES):
            load_wo(pool, k)

    def scalar(act):
        def split_h(b):
            act.wait_ge(h_landed, 16 * b + 16)
            if not isinstance(b, int) or b > 0:
                act.wait_ge(proj_done, NU * b)
            for i in range(4):
                cols = slice(i * 512, (i + 1) * 512)
                nc.scalar.activation(h_hi[:, 2 * i:2 * i + 2].rearrange("p k t -> p (k t)"), act_raw[:, cols],
                                     ACT.Copy).then_inc(h_hi_done, 1)

        def copy_k(b, j):
            act.wait_ge(proj_done, at(b, f"k{j}"))
            bank = UNITS.index(f"k{j}") % 2
            for i in range(4):
                for q in (0, 1):
                    ins = nc.scalar.activation(k_stack[32 * q:32 * q + 32, 4 * j + i],
                                               psP[32 * i:32 * i + 32, bank, 0:T], ACT.Copy)
            ins.then_inc(proj_act, 1)

        def copy_v(b, t):
            act.wait_ge(proj_done, at(b, f"v{t}"))
            v = psP[:, t, 0:NKV].rearrange("p (g d) -> p g d", g=G)
            nc.scalar.activation(v_pad[:, t, 0:4, HD:2 * HD], v[:, 0:4], ACT.Copy).then_inc(proj_act, 1)

        def copy_q(b, g, hp):
            bank = UNITS.index(f"q{g}") % 2
            if hp == 0:
                act.wait_ge(proj_done, at(b, f"q{g}"))
            for h in (2 * hp, 2 * hp + 1):
                ins = nc.scalar.activation(q_stack[0:32, g % 4, h], psP[32 * h:32 * h + 32, bank, 0:T], ACT.Copy)
            ins.then_inc(proj_act if hp else q_hi_done, 1)

        def exp(n, g, i):
            act.wait_ge(st_done, TILES * n + i + 1)
            if i == 0 and live(n - 2):
                act.wait_ge(pv_done, 2 * (n - 1))
            nc.scalar.activation(probs[:, g % 2, i % 2, (i // 2) * 512:(i // 2 + 1) * 512], psT[:, i % 2],
                                 ACT.Exp, scale=ATT_SCALE).then_inc(exp_done, 1)

        def step(n, g, b):
            if isinstance(n, int) and n < G:
                for i in SPLIT_AT[g]:
                    weights.split_hi(act, W_TILES + i, wq[:, i, 0])
            if live(n) and g == 0:
                copy_k(b, 0)
            for hp in range(2):
                if live(n - 2):
                    for i in (2 * hp, 2 * hp + 1):
                        exp(n - 2, g, i)
                if hp == 1 and live(n - 1):
                    act.wait_ge(turned, n)
                    nc.scalar.activation(nmax_rows[:, (g - 1) % 2], psM[0:16, 0:P], ACT.Copy).then_inc(rows_done, 1)
                if live(n):
                    copy_q(b, g, hp)
            if live(n) and g == 2:
                if live(n - G):
                    act.wait_ge(pv_done, 2 * G * b)
                for t in range(2):
                    copy_v(b, t)
            if live(n) and g == 3:
                copy_k(b, 1)
            if g == G - 1 and has_next(b):
                split_h(b + 1)

        split_h(0)
        act.wait_ge(filled, 3)
        act.wait_ge(before.h_done, before.tiles)
        run(act, step, True)

    def vector(dve):
        def split_h(b):
            for i in range(4):
                dve.wait_ge(h_hi_done, 4 * b + i + 1)
                cols = slice(i * 512, (i + 1) * 512)
                dve.tensor_tensor(h_lo[:, 2 * i:2 * i + 2].rearrange("p k t -> p (k t)"), act_raw[:, cols],
                                  f(h_hi[:, 2 * i:2 * i + 2].rearrange("p k t -> p (k t)")),
                                  ALU.subtract).then_inc(h_lo_done, 1)

        def copy_k(b, j):
            dve.wait_ge(proj_act, at(b, f"k{j}"))
            bank = UNITS.index(f"k{j}") % 2
            for i in range(4):
                kv = 4 * j + i
                ins = dve.tensor_tensor(k_stack[64:96, kv], psP[32 * i:32 * i + 32, bank, 0:T],
                                        f(k_stack[0:32, kv]), ALU.subtract)
            ins.then_inc(proj_dve, 1)

        def copy_v(b, t):
            dve.wait_ge(proj_act, at(b, f"v{t}"))
            v = psP[:, t, 0:NKV].rearrange("p (g d) -> p g d", g=G)
            dve.tensor_copy(v_pad[:, t, 4:8, HD:2 * HD], v[:, 4:8]).then_inc(proj_dve, 1)

        def copy_q(b, n, g, hp):
            bank = UNITS.index(f"q{g}") % 2
            if hp:
                dve.wait_ge(proj_act, at(b, f"q{g}"))
            else:
                dve.wait_ge(q_hi_done, n + 1)
            two = slice(2 * hp, 2 * hp + 2)
            for h in (2 * hp, 2 * hp + 1):
                ins = dve.tensor_tensor(q_stack[32:64, g % 4, h], psP[32 * h:32 * h + 32, bank, 0:T],
                                        f(q_stack[0:32, g % 4, h]), ALU.subtract)
            if hp:
                ins.then_inc(proj_dve, 1)
            dve.tensor_copy(q_stack[64:96, g % 4, two], q_stack[0:32, g % 4, two]).then_inc(q_ready, 1)

        def maxima(n, g):
            for i in range(TILES):
                hp, qt = i // 2, i % 2
                dve.wait_ge(s_done, TILES * n + i + 1)
                dve.tensor_reduce(nmax[:, g % 2, 2 * hp:2 * hp + 2, qt],
                                  psS[:, i % 2].rearrange("p (h k) -> p h k", h=2),
                                  AX.X, ALU.max, negate=True).then_inc(s_max, 1)
            flat = nmax[:, g % 2].rearrange("p h q -> p (h q)")
            dve.wait_ge(s_max, TILES * (n + 1))
            dve.tensor_copy(nmax_parts[:, g % 2, 0:8], flat).then_inc(nmax_hi, 1)
            dve.wait_ge(nmax_hi, n + 1)
            dve.tensor_tensor(nmax_parts[:, g % 2, 8:16], flat, f(nmax_parts[:, g % 2, 0:8]),
                              ALU.subtract).then_inc(nmax_lo, 1)

        def copy_o(n, g, b):
            dve.wait_ge(pv_done, 2 * n + 2)
            if live(n - 4):
                dve.wait_ge(o_stored[g % 4], 32 * (2 * b + g // 4))
            dve.tensor_copy(o_sb[:, g % 4], psO[:]).then_inc(o_copied, 1)

        def step(n, g, b):
            if isinstance(n, int) and n < G:
                for i in SPLIT_AT[g]:
                    weights.split_lo(dve, W_TILES + i, wq[:, i, 0], wq[:, i, 1])
            if live(n) and g == 0:
                copy_k(b, 0)
            if live(n - 1):
                maxima(n - 1, (g - 1) % G)
            for hp in range(2):
                if live(n):
                    copy_q(b, n, g, hp)
            if live(n - 3):
                copy_o(n - 3, (g - 3) % G, b if g >= 3 else b - 1)
            if live(n) and g == 2:
                for t in range(2):
                    copy_v(b, t)
            if live(n) and g == 3:
                copy_k(b, 1)
            if g == G - 1 and has_next(b):
                split_h(b + 1)

        split_h(0)
        dve.wait_ge(filled, 3)
        run(dve, step, True)

    def tensor(pe):
        def project(b, unit, half=None):
            u = UNITS.index(unit)
            if half in (None, 0) and not (isinstance(b, int) and b == 0 and u < 2):
                pe.wait_ge(proj_act, NU * b + u - 1)
                pe.wait_ge(proj_dve, NU * b + u - 1)
            out = psP[:, u % 2, 0:T]
            kind, j = unit[0], int(unit[1])
            if isinstance(b, int) and b == 0:
                pe.wait_ge(weights.lo_done, W_TILES + (6 if kind == "v" else u + 1))
            for k in range(KT) if half is None else range(4 * half, 4 * half + 4):
                if unit == "k0" and k % 2 == 0:
                    pe.wait_ge(h_lo_done, 4 * b + k // 2 + 1)
                for i, (w, h) in enumerate(((0, h_hi), (0, h_lo), (1, h_hi))):
                    first, end = k == 0 and i == 0, k == KT - 1 and i == 2
                    if kind == "v":
                        mm = pe.matmul(out, h[:, k, j * P:(j + 1) * P], wq[:, 4:6, w, k * P:(k + 1) * P],
                                       start=first, stop=end)
                    else:
                        mm = pe.matmul(out, wq[:, u, w, k * P:(k + 1) * P], h[:, k], start=first, stop=end)
            if half in (None, 1):
                mm.then_inc(proj_done, 1)

        def scores(n, g, i):
            hp, qt = i // 2, i % 2
            if qt == 0:
                pe.wait_ge(q_ready, 2 * n + hp + 1)
            if i >= 2 or live(n - 1):
                pe.wait_ge(s_max, TILES * n + i - 1)
            for j in range(2):
                mm = pe.matmul(psS[:, i % 2, j * T:(j + 1) * T],
                               q_stack[0:96, g % 4, 2 * hp + j, qt * P:(qt + 1) * P], k_stack[0:96, g],
                               start=True, stop=True)
            mm.then_inc(s_done, 1)

        def scores_t(n, g, i):
            hp, kt = i // 2, i % 2
            if i == 0:
                pe.wait_ge(rows_landed, 32 * n + 32)
            if i >= 2 or live(n - 1):
                pe.wait_ge(exp_done, TILES * n + i - 1)
            pe.matmul(psT[:, kt], k_stack[0:98, g, kt * P:(kt + 1) * P],
                      q_stack[0:98, g % 4, 2 * hp:2 * hp + 2].rearrange("p h t -> p (h t)"),
                      start=True, stop=True).then_inc(st_done, 1)

        def outputs(n, g, b, hp):
            if hp == 0:
                pe.wait_ge(exp_done, TILES * (n + 1))
                if live(n - 1):
                    pe.wait_ge(o_copied, n)
                if g == 0:
                    pe.wait_ge(proj_act, at(b, "v1"))
                    pe.wait_ge(proj_dve, at(b, "v1"))
            for i in range(2):
                c = HD * (1 - i)
                for kt in range(KK):
                    mm = pe.matmul(psO[:, hp], v_pad[:, kt, g, c:c + P],
                                   probs[:, g % 2, kt, (2 * hp + i) * T:(2 * hp + i + 1) * T],
                                   start=(i == 0 and kt == 0), stop=(i == 1 and kt == 1))
            mm.then_inc(pv_done, 1)

        def turn(n, g):
            pe.wait_ge(nmax_lo, n + 1)
            pe.transpose(psM[0:16, 0:P], f(nmax_parts[:, g % 2]), id_sb[:]).then_inc(turned, 1)

        def step(n, g, b):
            if live(n) and g == 0:
                project(b, "k0")
            for half in range(2):
                if live(n):
                    project(b, f"q{g}", half)
                if live(n - 1):
                    if g == 1 and half == 0:
                        pe.wait_ge(proj_dve, at(b, "k0"))
                    if g == 5 and half == 0:
                        pe.wait_ge(proj_dve, at(b, "k1"))
                    for i in (2 * half, 2 * half + 1):
                        scores(n - 1, (g - 1) % G, i)
            for hp in range(2):
                if live(n - 2):
                    for i in (2 * hp, 2 * hp + 1):
                        scores_t(n - 2, (g - 2) % G, i)
                if hp == 1 and live(n - 1):
                    turn(n - 1, (g - 1) % G)
                if live(n - 3):
                    outputs(n - 3, (g - 3) % G, b, hp)
            if live(n) and g == 2:
                project(b, "v0")
                project(b, "v1")
            if live(n) and g == 3:
                project(b, "k1")

        pe.wait_ge(before.h_copied, before.tiles)
        pe.wait_ge(id_landed, 16)
        pe.wait_ge(filled, 3)
        run(pe, step, False)

    st.sync, st.gpsimd, st.scalar, st.vector, st.tensor = sync, gpsimd, scalar, vector, tensor
    return st



def finish(nc, xT, oT, den, rden, Wo, idx, cond2, RA, ffn_B, ident, outT):
    ROWS = 4
    with ExitStack() as ctx:
        def sb(name, shape, dt=F32):
            return ctx.enter_context(nc.sbuf_tensor(name, shape, dt))

        def psum(name, shape):
            return ctx.enter_context(nc.psum_tensor(name, shape, F32))

        def sem(name):
            return ctx.enter_context(nc.semaphore(name))

        id_sb = sb("id_sb3", [P, P])
        idx_sb = sb("idx_sb3", [1, B], I32)
        ra_sb = sb("ra_sb", [P, KT, EC])
        fb_sb = sb("fb_sb", [ER, D])
        wo_raw = sb("wo_raw", [P, 2, D])
        wo_hi, wo_lo = sb("wo_hi", [P, KT, D], F32R), sb("wo_lo", [P, KT, D], F32R)
        o_raw = sb("o_raw", [P, 2, G, T])
        o_scale = sb("o_scale", [P, 2, G, T])
        den_sb = sb("den_sb3", [P, 2, 64])
        rden_sb = sb("rden_sb3", [P, 2, 64])
        o_hi, o_lo = sb("o_hi", [P, 2, G, T], F32R), sb("o_lo", [P, 2, G, T], F32R)
        x_sb = sb("x_sb", [P, 2, KT, T])
        cond = sb("cond", [P, ROWS, D])
        g_sb = sb("g_sb", [EC, D])
        g_t = sb("g_t", [P, KT, EC])
        mid = sb("mid", [P, 2, EC])
        rank0 = sb("rank0", [P, 2, E])
        rank = sb("rank", [P, 2, E])
        beats = sb("beats", [P, 2, E])
        top = sb("top", [P, 2])
        gate = sb("gate", [P, 2, E])
        gsum = sb("gsum", [P, 2])
        gated = sb("gated", [P, 2, EC])
        gated_t = sb("gated_t", [ER, T])

        psW = psum("psW", [P, 2, 512])
        psG = psum("psG", [P, 2, 512])
        psX = psum("psX", [P, 512])
        psY = psum("psY", [P, 2, 512])

        const_landed = sem("const_landed")
        wo_landed = [sem(f"wo_landed{i}") for i in range(2)]
        wo_hi_done, wo_lo_done = sem("wo_hi_done"), sem("wo_lo_done")
        den_landed, rden_done, rden_stored = sem("den_landed"), sem("rden_done"), sem("rden_stored")
        in_landed, x_landed = sem("o_landed"), sem("x_landed")
        o_scaled, o_hi_done, o_lo_done = sem("o_scaled"), sem("o_hi_done"), sem("o_lo_done")
        wo_done, x2_done = sem("wo_done"), sem("x2_done")
        cond_landed = [sem(f"cond_landed{i}") for i in range(ROWS)]
        cond_used = sem("cond_used")
        g_copied = sem("g_copied")
        gt_done, gt_copied = sem("gt_done"), sem("gt_copied")
        mid_done, mid_copied = sem("mid_done"), sem("mid_copied")
        chain = sem("chain")
        shifted, exp_done = sem("shifted"), sem("gate_exp_done")
        gated_done, turned, turned_copied = sem("gated_done"), sem("gated_turned"), sem("turned_copied")
        y_done, y_added = sem("y_done"), sem("y_added")
        stored = sem("stored")
        block = ctx.enter_context(nc.Block())

        @block.sync
        def _(sp):
            for dst, src in ((id_sb[:], ident), (idx_sb[:], idx), (ra_sb[:], RA), (fb_sb[:], ffn_B)):
                sp.dma_start(dst, src).then_inc(const_landed, 16)
            for k in range(KT):
                if k >= 2:
                    sp.wait_ge(wo_lo_done, k - 1)
                sp.dma_start(wo_raw[:, k % 2], Wo[k * P:(k + 1) * P]).then_inc(wo_landed[k % 2], 16)

            def load_o(pair):
                two = bass.ds(2 * pair, 2)
                sp.dma_start(den_sb[:], den[two].rearrange("b c g h t -> b (c g h t)")
                             .rearrange("b (p n) -> p b n", p=P)).then_inc(den_landed, 16)
                sp.dma_start(o_raw[:], oT[two].rearrange("b p g t -> p b (g t)")).then_inc(in_landed, 16)
                sp.wait_ge(rden_done, pair + 1)
                sp.dma_start(rden[two].rearrange("b c g h t -> b (c g h t)")
                             .rearrange("b (p n) -> p b n", p=P), rden_sb[:]).then_inc(rden_stored, 16)
                sp.wait_ge(rden_stored, 16 * pair + 16)
                for h in range(HG):
                    for c in range(2):
                        src = rden[bass.ds(2 * pair + c, 1), h % 2, :, h // 2].to_broadcast([32, G, T])
                        sp.dma_start(o_scale[32 * h:32 * h + 32, c], src).then_inc(in_landed, 16)

            def load_x(pair):
                sp.dma_start(x_sb[:], xT[bass.ds(2 * pair, 2)].rearrange("b p k t -> p b (k t)")
                             ).then_inc(x_landed, 16)

            def store(pair):
                sp.wait_ge(y_added, 2 * KT * pair + 2 * KT + 2)
                sp.dma_start(outT[bass.ds(2 * pair, 2)].rearrange("b p k t -> p b (k t)"), x_sb[:]
                             ).then_inc(stored, 16)
                sp.wait_ge(stored, 16 * pair + 16)

            load_o(0)
            load_x(0)
            with sp.Fori(0, PAIRS - 1) as pair:
                sp.wait_ge(o_lo_done, pair + 1)
                load_o(pair + 1)
                store(pair)
                load_x(pair + 1)
            store(PAIRS - 1)

        @block.gpsimd
        def _(pool):
            pool.wait_ge(const_landed, 64)
            for s in range(ROWS):
                slot = pool.value_load(idx_sb[0:1, 0:1], min_val=0, max_val=7)
                pool.dma_start(cond[:, s], cond2[bass.ds(slot, 1), s].rearrange("s p d -> (s p) d")
                               ).then_inc(cond_landed[s], 16)

            def rows(n):
                slot = pool.value_load(idx_sb[0:1, bass.ds(n, 1)], min_val=0, max_val=7)
                for k in range(ROWS, KT):
                    pool.wait_ge(cond_used, KT * n + k - ROWS + 1)
                    pool.dma_start(cond[:, k % ROWS], cond2[bass.ds(slot, 1), k].rearrange("s p d -> (s p) d")
                                   ).then_inc(cond_landed[k % ROWS], 16)

            def next_rows(n):
                slot = pool.value_load(idx_sb[0:1, bass.ds(n + 1, 1)], min_val=0, max_val=7)
                for k in range(ROWS):
                    pool.wait_ge(cond_used, KT * n + KT - ROWS + k + 1)
                    pool.dma_start(cond[:, k], cond2[bass.ds(slot, 1), k].rearrange("s p d -> (s p) d")
                                   ).then_inc(cond_landed[k], 16)

            with pool.Fori(0, PAIRS - 1) as pair:
                rows(2 * pair)
                next_rows(2 * pair)
                rows(2 * pair + 1)
                next_rows(2 * pair + 1)
            rows(B - 2)
            next_rows(B - 2)
            rows(B - 1)

        @block.scalar
        def _(act):
            act.sem_inc(g_copied, 1)
            for k in range(KT):
                act.wait_ge(wo_landed[k % 2], 16 * (k // 2 + 1))
                nc.scalar.activation(wo_hi[:, k], wo_raw[:, k % 2], ACT.Copy).then_inc(wo_hi_done, 1)

            def split_o(pair):
                act.wait_ge(o_scaled, pair + 1)
                nc.scalar.activation(o_hi[:], o_raw[:], ACT.Copy).then_inc(o_hi_done, 1)

            def batch(n):
                act.wait_ge(cond_used, KT * (n + 1))
                nc.scalar.activation(g_sb[:], psG[0:EC].rearrange("p a b -> p (a b)"), ACT.Copy).then_inc(g_copied, 1)
                act.wait_ge(shifted, n + 1)
                nc.scalar.activation(gate[:], beats[:], ACT.Exp).then_inc(exp_done, 1)
                act.wait_ge(turned, n + 1)
                nc.scalar.activation(gated_t[:], psX[0:ER, 0:T], ACT.Copy, scale=FFN_SCALE).then_inc(turned_copied, 1)

            split_o(0)
            with act.Fori(0, PAIRS - 1) as pair:
                for c in range(2):
                    batch(2 * pair + c)
                split_o(pair + 1)
            for c in range(2):
                batch(B - 2 + c)

        @block.vector
        def _(dve):
            dve.sem_inc(x2_done, 2)
            dve.sem_inc(y_added, 2)
            dve.memset(gated[:, :, ER:EC], 0.0)
            for e in range(E):
                ins = dve.memset(rank0[:, :, e:e + 1], float(e))
            ins.then_inc(chain, 1)
            for k in range(KT):
                dve.wait_ge(wo_hi_done, k + 1)
                dve.tensor_tensor(wo_lo[:, k], wo_raw[:, k % 2], f(wo_hi[:, k]), ALU.subtract).then_inc(wo_lo_done, 1)

            def split_o(pair):
                dve.wait_ge(den_landed, 16 * pair + 16)
                dve.reciprocal(rden_sb[:], den_sb[:]).then_inc(rden_done, 1)
                dve.wait_ge(in_landed, 16 * 9 * (pair + 1))
                dve.tensor_tensor(o_raw[:], o_raw[:], o_scale[:], ALU.mult).then_inc(o_scaled, 1)
                dve.wait_ge(o_hi_done, pair + 1)
                dve.tensor_tensor(o_lo[:], o_raw[:], f(o_hi[:]), ALU.subtract).then_inc(o_lo_done, 1)

            def residual(pair):
                dve.wait_ge(x_landed, 16 * pair + 16)
                for m in range(KT):
                    dve.wait_ge(wo_done, KT * pair + m + 1)
                    dve.tensor_tensor(x_sb[:, :, m], x_sb[:, :, m],
                                      psW[:, m % 2].rearrange("p (b t) -> p b t", b=2), ALU.add).then_inc(x2_done, 1)

            CH = 15

            def batch(n):
                done = [0]

                def step(ins):
                    done[0] += 1
                    ins.then_inc(chain, 1)
                    dve.wait_ge(chain, CH * n + done[0] + 1)

                dve.wait_ge(gt_done, 2 * n + 1)
                dve.tensor_copy(g_t[:, 0:4], psX[:, 0:4 * EC].rearrange("p (k e) -> p k e", k=4)).then_inc(gt_copied, 1)
                dve.wait_ge(gt_done, 2 * n + 2)
                dve.tensor_copy(g_t[:, 4:8], psX[:, 0:4 * EC].rearrange("p (k e) -> p k e", k=4)).then_inc(gt_copied, 1)
                dve.wait_ge(mid_done, n + 1)
                step(dve.tensor_copy(mid[:], psX[:, 0:2 * EC].rearrange("p (t e) -> p t e", t=2)))
                logit = mid[:, :, ER:EC]
                for d in range(1, E):
                    step(dve.tensor_tensor(beats[:, :, 0:E - d], logit[:, :, d:E], logit[:, :, 0:E - d], ALU.is_gt))
                    if d == 1:
                        step(dve.tensor_copy(rank[:], rank0[:]))
                    step(dve.tensor_tensor(rank[:, :, 0:E - d], rank[:, :, 0:E - d], beats[:, :, 0:E - d], ALU.add))
                    step(dve.tensor_tensor(rank[:, :, d:E], rank[:, :, d:E], beats[:, :, 0:E - d], ALU.subtract))
                step(dve.tensor_reduce(top[:], logit, AX.X, ALU.max))
                for t in range(2):
                    ins = dve.tensor_scalar(beats[:, t], logit[:, t], top[:, t:t + 1], None, ALU.subtract)
                ins.then_inc(shifted, 1)
                dve.wait_ge(exp_done, n + 1)
                step(dve.scalar_tensor_tensor(gate[:], rank[:], 1.5, gate[:], ALU.is_lt, ALU.mult))
                step(dve.tensor_reduce(gsum[:], gate[:], AX.X, ALU.add))
                dve.reciprocal(gsum[:], gsum[:]).then_inc(chain, 1)
                dve.wait_ge(chain, CH * n + CH + 1)
                for t in range(2):
                    for e in range(E):
                        ins = dve.tensor_scalar(gated[:, t, e * R:(e + 1) * R], mid[:, t, e * R:(e + 1) * R],
                                                gate[:, t, e:e + 1], gsum[:, t:t + 1], ALU.mult, ALU.mult)
                ins.then_inc(gated_done, 1)
                assert done[0] + 1 == CH
                for m in range(KT):
                    dve.wait_ge(y_done, KT * n + m + 1)
                    c = n_parity[0]
                    dve.tensor_tensor(x_sb[:, c, m], x_sb[:, c, m], psY[:, m % 2, 0:T], ALU.add).then_inc(y_added, 1)

            n_parity = [0]
            split_o(0)
            with dve.Fori(0, PAIRS - 1) as pair:
                residual(pair)
                for c in range(2):
                    n_parity[0] = c
                    batch(2 * pair + c)
                split_o(pair + 1)
            residual(PAIRS - 1)
            for c in range(2):
                n_parity[0] = c
                batch(B - 2 + c)

        @block.tensor
        def _(pe):
            pe.wait_ge(wo_lo_done, KT)
            pe.wait_ge(const_landed, 64)
            with pe.Fori(0, PAIRS) as pair:
                pe.wait_ge(o_lo_done, pair + 1)
                for m in range(KT):
                    pe.wait_ge(x2_done, KT * pair + m + 1)
                    cols = slice(m * P, (m + 1) * P)
                    n = 0
                    for k in range(KT):
                        for w, o in ((wo_hi, o_hi), (wo_hi, o_lo), (wo_lo, o_hi)):
                            mm = pe.matmul(psW[:, m % 2].rearrange("p (b t) -> p b t", b=2), w[:, k, cols],
                                           o[:, :, k], start=(n == 0), stop=(n == 3 * KT - 1))
                            n += 1
                    mm.then_inc(wo_done, 1)
                for c in range(2):
                    nb = 2 * pair + c
                    pe.wait_ge(g_copied, nb + 1)
                    for k in range(KT):
                        pe.wait_ge(cond_landed[k % ROWS], 16 * (2 * nb + k // ROWS + 1))
                        for half in range(2):
                            mm = pe.matmul(psG[0:EC, half], ra_sb[:, k], cond[:, k % ROWS, half * 512:(half + 1) * 512],
                                           start=(k == 0), stop=(k == KT - 1))
                        mm.then_inc(cond_used, 1)
                    pe.wait_ge(g_copied, nb + 2)
                    for half in range(2):
                        if half == 1:
                            pe.wait_ge(gt_copied, 2 * nb + 1)
                        for k in range(4):
                            kk = 4 * half + k
                            mm = pe.transpose(psX[:, k * EC:(k + 1) * EC], g_sb[:, kk * P:(kk + 1) * P],
                                              id_sb[0:EC, 0:EC])
                        mm.then_inc(gt_done, 1)
                    pe.wait_ge(x2_done, KT * pair + KT + 2)
                    pe.wait_ge(gt_copied, 2 * nb + 2)
                    for t in range(2):
                        for k in range(KT):
                            mm = pe.matmul(psX[:, t * EC:(t + 1) * EC], x_sb[:, c, k, t * P:(t + 1) * P], g_t[:, k],
                                           start=(k == 0), stop=(k == KT - 1))
                    mm.then_inc(mid_done, 1)
                    pe.wait_ge(gated_done, nb + 1)
                    for t in range(2):
                        mm = pe.transpose(psX[0:EC, t * P:(t + 1) * P], gated[:, t], id_sb[:])
                    mm.then_inc(turned, 1)
                    pe.wait_ge(turned_copied, nb + 1)
                    for m in range(KT):
                        pe.wait_ge(y_added, KT * nb + m + 1)
                        pe.matmul(psY[:, m % 2, 0:T], fb_sb[:, m * P:(m + 1) * P], gated_t[:],
                                  start=True, stop=True).then_inc(y_done, 1)


_INS = ["xT", "itok_A", "itok_C", "WT", "bias", "lora_A", "lora_B", "Wqkv", "Wo", "cond2", "RA", "ffn_B", "ident"]


def build(nc, a, outT):
    hT = nc.dram_tensor("h_scratch", (B, P, KT, T), F32).ap()
    oT = nc.dram_tensor("o_scratch", (B, P, G, T), F32).ap()
    den = nc.dram_tensor("den_scratch", (B, 2, G, 2, T), F32).ap()
    rden = nc.dram_tensor("rden_scratch", (B, 2, G, 2, T), F32).ap()
    COLS = [D, 0, P, 2 * P, D + NKV, D + NKV + P, 3 * P, D + P, 4 * P, 5 * P, 6 * P, 7 * P]

    def load_qkv(eng, i):
        weights.load(eng, W_TILES + i, a["Wqkv"][:, COLS[i]:COLS[i] + P].rearrange("(k p) c -> p k c", p=P))

    def load_wo(eng, k):
        pass

    with ExitStack() as ctx:
        def sb(name, shape, dt=F32):
            return ctx.enter_context(nc.sbuf_tensor(name, shape, dt))

        def sem(name):
            return ctx.enter_context(nc.semaphore(name))

        weights = Weights(nc, sb, sem)
        act_raw = sb("act_raw", [P, KT * T])
        with nc.sbuf_tensor("wq", [P, QKV_TILES, 2, D], F32R) as wq:
            pass
        tokens = tokens_stage(nc, sem, weights, wq, load_qkv, a["xT"], a["itok_A"], a["WT"], a["bias"], a["lora_A"],
                              a["lora_B"], hT)
        attend = attend_stage(nc, sem, weights, wq, act_raw, load_qkv, load_wo, tokens, a["ident"], hT, oT, den)
        with nc.Block() as block:
            @block.sync
            def _(sp):
                tokens.sync(sp)
                attend.sync(sp)
                for s in attend.o_stored:
                    sp.wait_ge(s, attend.o_all)

            @block.gpsimd
            def _(pool):
                tokens.gpsimd(pool)
                attend.gpsimd(pool)

            @block.scalar
            def _(act):
                tokens.scalar(act)
                attend.scalar(act)

            @block.vector
            def _(dve):
                tokens.vector(dve)
                attend.vector(dve)

            @block.tensor
            def _(pe):
                tokens.tensor(pe)
                attend.tensor(pe)
    finish(nc, a["xT"], oT, den, rden, a["Wo"], a["itok_C"], a["cond2"], a["RA"], a["ffn_B"], a["ident"], outT)


def kernel(x, itok_B_0_23, itok_B_3_7, L0_cond_W, L0_cond_b, L0_cond_lora_As, L0_cond_lora_Bs, L0_attn_w_q,
           L0_attn_w_k, L0_attn_w_v, L0_attn_w_o, L0_cond2_weight, L0_ffn_router_w, L0_ffn_A, L0_ffn_B):
    import concourse.bacc as _bacc
    from concourse.bass_utils import run_bass_kernel_spmd as _run

    def tiles(a):
        a = a.reshape(a.shape[:-2] + (KT, P, a.shape[-1]))
        return np.swapaxes(a, -3, -2)

    x = np.asarray(x)
    arrays = {
        "xT": tiles(np.swapaxes(x, 1, 2)),
        "itok_A": np.asarray(itok_B_0_23).reshape(1, B),
        "itok_C": np.asarray(itok_B_3_7).reshape(1, B),
        "WT": tiles(np.asarray(L0_cond_W).T),
        "bias": np.asarray(L0_cond_b).reshape(KT, P).T,
        "lora_A": tiles(np.asarray(L0_cond_lora_As)),
        "lora_B": np.asarray(L0_cond_lora_Bs),
        "Wqkv": np.concatenate([np.asarray(w) for w in (L0_attn_w_q, L0_attn_w_k, L0_attn_w_v)], axis=1),
        "Wo": np.asarray(L0_attn_w_o),
        "cond2": np.asarray(L0_cond2_weight).reshape(-1, KT, P, D),
        "RA": tiles(np.concatenate([np.asarray(L0_ffn_A).reshape(ER, D), np.asarray(L0_ffn_router_w)], axis=0).T),
        "ffn_B": np.swapaxes(np.asarray(L0_ffn_B), 1, 2).reshape(ER, D),
        "ident": np.eye(P, dtype=np.float32),
    }
    nc = _bacc.Bacc("TRN2", target_bir_lowering=False, num_devices=1)
    aps, sent = {}, {}
    for name in _INS:
        v = np.ascontiguousarray(arrays[name])
        sent[f"in_{name}"] = v
        aps[name] = nc.dram_tensor(f"in_{name}", v.shape, mybir.dt.from_np(v.dtype), kind="ExternalInput").ap()
    outT = nc.dram_tensor("outT", (B, P, KT, T), F32, kind="ExternalOutput").ap()
    build(nc, aps, outT)
    r = _run(nc, [sent], core_ids=[0])
    out = r.results[0]["outT"]
    return np.ascontiguousarray(out.transpose(0, 3, 2, 1).reshape(B, T, D))
```

```python
from contextlib import ExitStack

import numpy as np

import concourse.bass as bass
from concourse import mybir

P = 128
B, T, D = 8, 256, 1024
KT = D // P
H, G, HD = 32, 8, 32
HG = H // G
NKV = G * HD
NQKV = D + 2 * NKV
R = 16
LORA_SCALE = 2.0
E = 4
ER = E * R
EC = ER + E
FFN_SCALE = 4.0
T2 = 2 * T
PAIRS = B // 2
ATT_SCALE = float(HD) ** -0.5

F32 = mybir.dt.float32
F32R = mybir.dt.float32r
I32 = mybir.dt.int32
ACT = mybir.ActivationFunctionType
ALU = mybir.AluOpType
AX = mybir.AxisListType

RING = 3
W_TILES = KT
QKV_TILES = NQKV // P
WO_TILES = KT


def f(ap):
    return ap.bitcast(F32)


class Weights:

    def __init__(self, nc, sb, sem):
        self.nc = nc
        self.raw = sb("weight_raw", [P, RING, D])
        self.landed = [sem(f"weight_landed{i}") for i in range(RING)]
        self.hi_done = sem("weight_hi_done")
        self.lo_done = sem("weight_lo_done")

    def load(self, eng, n, src):
        if n >= RING:
            eng.wait_ge(self.lo_done, n - RING + 1)
        dst = self.raw[:, n % RING]
        if len(src.shape) == 3:
            dst = dst.rearrange("p (k c) -> p k c", c=src.shape[2])
        eng.dma_start(dst, src).then_inc(self.landed[n % RING], 16)

    def split_hi(self, act, n, hi):
        act.wait_ge(self.landed[n % RING], 16 * (n // RING + 1))
        self.nc.scalar.activation(hi, self.raw[:, n % RING], ACT.Copy).then_inc(self.hi_done, 1)

    def split_lo(self, dve, n, hi, lo):
        dve.wait_ge(self.hi_done, n + 1)
        dve.tensor_tensor(lo, self.raw[:, n % RING], f(hi), ALU.subtract).then_inc(self.lo_done, 1)


class Stage:
    pass


def tokens_stage(nc, sem, weights, wq, ahead, load_qkv, xT, idx, WT, bias, lora_A, lora_B, hT):
    SLOTS = 4
    BANK = [0, 1, 2, 3, 4, 5, 6, 3]
    AB_DMAS = 8
    st = Stage()
    with ExitStack() as ctx:
        def sb(name, shape, dt=F32):
            return ctx.enter_context(nc.sbuf_tensor(name, shape, dt))

        sb("qkv_head", [P, 4, 2, D])
        w_hi, w_lo = sb("w_hi", [P, KT, D], F32R), sb("w_lo", [P, KT, D], F32R)
        x_raw = sb("x_raw", [P, KT, T2])
        x_hi, x_lo = sb("x_hi", [P, KT, T2], F32R), sb("x_lo", [P, KT, T2], F32R)
        idx_sb = sb("idx_sb", [1, B], I32)
        bias_sb = sb("bias_sb", [P, KT])
        a_raw = sb("a_raw", [P, 2, KT, R])
        a_hi, a_lo = sb("a_hi", [P, 2, KT, R], F32R), sb("a_lo", [P, 2, KT, R], F32R)
        b_raw = sb("b_raw", [96, 2, D])
        b_stack = sb("b_stack", [96, 2, D], F32R)
        u_stack = sb("u_stack", [96, 2, T], F32R)
        h_out = sb("h_out", [P, SLOTS, T2])
        psH = ctx.enter_context(nc.psum_tensor("psH", [P, 7, T2], F32))
        psU = ctx.enter_context(nc.psum_tensor("psU", [P, T2], F32))

        idx_landed, bias_landed = sem("idx_landed"), sem("bias_landed")
        x_landed = [sem(f"x_landed{k}") for k in range(KT)]
        ab_landed = sem("ab_landed")
        zeroed = sem("zeroed")
        x_hi_done, x_lo_done, x_used = sem("x_hi_done"), sem("x_lo_done"), sem("x_used")
        ab_hi_done, ab_lo_done = sem("ab_hi_done"), sem("ab_lo_done")
        u_done, u_hi_done, u_lo_done = sem("u_done"), sem("u_hi_done"), sem("u_lo_done")
        h_done, h_copied = sem("h_done"), sem("h_copied")
        h_stored = [sem(f"h_stored{i}") for i in range(SLOTS)]
        st.h_done, st.h_copied, st.h_stored, st.idx = h_done, h_copied, h_stored, idx_sb
        st.h_all = 16 * PAIRS * KT // SLOTS
        st.tiles = PAIRS * KT
        st.x_lo_done, st.x_splits = x_lo_done, PAIRS * KT

    def both(ap):
        return ap.rearrange("p (b t) -> p b t", b=2)

    def sync(sp):
        def load_x(pair, k):
            sp.dma_start(both(x_raw[:, k]), xT[bass.ds(2 * pair, 2), :, k].rearrange("b p t -> p b t")
                         ).then_inc(x_landed[k], 16)

        def load_ab(pair):
            for c in range(2):
                slot = sp.value_load(idx_sb[0:1, bass.ds(2 * pair + c, 1)], min_val=0, max_val=31)
                sp.dma_start(a_raw[:, c], lora_A[bass.ds(slot, 1)].rearrange("s p k r -> p (s k) r")
                             ).then_inc(ab_landed, 16)
                for q in range(3):
                    sp.dma_start(b_raw[32 * q:32 * q + R, c], lora_B[bass.ds(slot, 1)].rearrange("s r d -> (s r) d")
                                 ).then_inc(ab_landed, 16)

        def pair_program(pair, last):
            if not last:
                for k in range(KT):
                    sp.wait_ge(x_lo_done, KT * pair + k + 1)
                    load_x(pair + 1, k)
                sp.wait_ge(ab_lo_done, pair + 1)
                load_ab(pair + 1)
            else:
                ahead.sync(sp)
            for s in range(KT):
                dst = hT[bass.ds(2 * pair, 2), :, s].rearrange("b p t -> p b t")
                sp.wait_ge(h_copied, KT * pair + s + 1)
                sp.dma_start(dst, both(h_out[:, s % SLOTS])).then_inc(h_stored[s % SLOTS], 16)

        sp.dma_start(idx_sb[:], idx).then_inc(idx_landed, 16)
        for k in range(KT):
            load_x(0, k)
        sp.dma_start(bias_sb[:], bias).then_inc(bias_landed, 16)
        sp.wait_ge(idx_landed, 16)
        sp.wait_ge(zeroed, 1)
        load_ab(0)
        with sp.Fori(0, PAIRS - 1) as pair:
            pair_program(pair, False)
        pair_program(PAIRS - 1, True)

    def gpsimd(pool):
        for k in range(W_TILES):
            weights.load(pool, k, WT[:, k])
        for i in range(7):
            load_qkv(pool, i)

    def scalar(act):
        def split_x(pair, k):
            act.wait_ge(x_landed[k], 16 * pair + 16)
            if not isinstance(pair, int) or pair > 0:
                act.wait_ge(x_used, KT * (pair - 1) + k + 1)
            nc.scalar.activation(x_hi[:, k], x_raw[:, k], ACT.Copy).then_inc(x_hi_done, 1)

        def pair_program(pair, first, last):
            act.wait_ge(ab_landed, 16 * AB_DMAS * (pair + 1))
            nc.scalar.activation(a_hi[:], a_raw[:], ACT.Copy)
            nc.scalar.activation(b_stack[:], b_raw[:], ACT.Copy).then_inc(ab_hi_done, 1)
            act.wait_ge(u_done, pair + 1)
            for q in (0, 1):
                nc.scalar.activation(u_stack[32 * q:32 * q + R], both(psU[0:R]), ACT.Copy,
                                     scale=LORA_SCALE).then_inc(u_hi_done, 1)
            for s in range(KT):
                if s == 4:
                    if last:
                        for i in range(4):
                            weights.split_hi(act, W_TILES + i, wq[:, i, 0])
                        ahead.scalar(act)
                    else:
                        for k in range(KT):
                            split_x(pair + 1, k)
                act.wait_ge(h_done, KT * pair + s + 1)
                if s >= SLOTS or not first:
                    act.wait_ge(h_stored[s % SLOTS], 16 * (KT // SLOTS * pair + s // SLOTS))
                nc.scalar.activation(h_out[:, s % SLOTS], psH[:, BANK[s]], ACT.Identity,
                                     bias=bias_sb[:, s:s + 1]).then_inc(h_copied, 1)

        for k in range(KT):
            split_x(0, k)
            weights.split_hi(act, k, w_hi[:, k])
        act.wait_ge(bias_landed, 16)
        act.wait_ge(zeroed, 2)
        pair_program(0, True, False)
        with act.Fori(1, PAIRS - 1) as pair:
            pair_program(pair, False, False)
        pair_program(PAIRS - 1, False, True)

    def vector(dve):
        def split_x(pair, k):
            dve.wait_ge(x_hi_done, KT * pair + k + 1)
            dve.tensor_tensor(x_lo[:, k], x_raw[:, k], f(x_hi[:, k]), ALU.subtract).then_inc(x_lo_done, 1)

        def pair_program(pair, last):
            dve.wait_ge(ab_hi_done, pair + 1)
            dve.tensor_tensor(b_stack[32:64], b_raw[32:64], f(b_stack[32:64]), ALU.subtract)
            dve.tensor_tensor(a_lo[:], a_raw[:], f(a_hi[:]), ALU.subtract).then_inc(ab_lo_done, 1)
            dve.wait_ge(u_hi_done, 2 * pair + 2)
            dve.scalar_tensor_tensor(u_stack[64:64 + R], both(psU[0:R]), LORA_SCALE, f(u_stack[0:R]),
                                     ALU.mult, ALU.subtract).then_inc(u_lo_done, 1)
            if last:
                for i in range(4):
                    weights.split_lo(dve, W_TILES + i, wq[:, i, 0], wq[:, i, 1])
                ahead.vector(dve)
            else:
                for k in range(KT):
                    split_x(pair + 1, k)

        dve.memset(b_raw[:], 0.0).then_inc(zeroed, 1)
        dve.memset(f(u_stack[:]), 0.0).then_inc(zeroed, 1)
        for k in range(KT):
            split_x(0, k)
            weights.split_lo(dve, k, w_hi[:, k], w_lo[:, k])
        with dve.Fori(0, PAIRS - 1) as pair:
            pair_program(pair, False)
        pair_program(PAIRS - 1, True)

    def tensor(pe):
        def products(m, k, first):
            cols = slice(m * P, (m + 1) * P)
            for i, (w, x) in enumerate(((w_hi, x_hi), (w_hi, x_lo), (w_lo, x_hi))):
                mm = pe.matmul(psH[:, BANK[m]], w[:, k, cols], x[:, k], start=(first and i == 0), stop=False)
            return mm

        def low_rank(m):
            for c in range(2):
                mm = pe.matmul(psH[:, BANK[m], c * T:(c + 1) * T], b_stack[:, c, m * P:(m + 1) * P],
                               u_stack[:, c], start=False, stop=(c == 1))
            mm.then_inc(h_done, 1)

        def pair_program(pair, first):
            for k in range(KT):
                pe.wait_ge(x_lo_done, KT * pair + k + 1)
                if first:
                    pe.wait_ge(weights.lo_done, k + 1)
                if k == KT - 1:
                    pe.wait_ge(ab_lo_done, pair + 1)
                    for c in range(2):
                        n = 0
                        for kk in range(KT):
                            for a, x in ((a_hi, x_hi), (a_hi, x_lo), (a_lo, x_hi)):
                                mm = pe.matmul(psU[0:R, c * T:(c + 1) * T], a[:, c, kk],
                                               x[:, kk, c * T:(c + 1) * T], start=(n == 0), stop=(n == 3 * KT - 1))
                                n += 1
                    mm.then_inc(u_done, 1)
                for s in range(4):
                    if k == 0 and not first:
                        pe.wait_ge(h_copied, KT * pair if s == 3 else KT * (pair - 1) + s + 1)
                    products(s, k, k == 0)
            pe.wait_ge(u_lo_done, pair + 1)
            for s in range(4):
                low_rank(s)
            for k in range(KT):
                for s in range(4, KT):
                    if k == 0 and s == 7:
                        pe.wait_ge(h_copied, KT * pair + 4)
                    elif k == 0 and not first:
                        pe.wait_ge(h_copied, KT * (pair - 1) + s + 1)
                    mm = products(s, k, k == 0)
                mm.then_inc(x_used, 1)
            for s in range(4, KT):
                low_rank(s)

        pair_program(0, True)
        with pe.Fori(1, PAIRS) as pair:
            pair_program(pair, False)

    st.sync, st.gpsimd, st.scalar, st.vector, st.tensor = sync, gpsimd, scalar, vector, tensor
    return st


def attend_stage(nc, sem, weights, wq, act_raw, load_qkv, load_wo, before, ahead_here, ahead, id_sb,
                 ident, hT, oT, den):
    KK = 2
    N = B * G
    TILES = 4
    UNITS = ["k0", "q0", "q1", "q2", "v0", "v1", "q3", "k1", "q4", "q5", "q6", "q7"]
    NU = len(UNITS)
    SPLIT_AT = [[4, 5], [6, 7], [8], [9], [10], [11], [], []]
    st = Stage()
    with ExitStack() as ctx:
        def sb(name, shape, dt=F32):
            return ctx.enter_context(nc.sbuf_tensor(name, shape, dt))

        def psum(name, shape):
            return ctx.enter_context(nc.psum_tensor(name, shape, F32))

        sb("qkv_all", [P, QKV_TILES, 2, D])
        h_hi, h_lo = sb("h_hi", [P, KT, T], F32R), sb("h_lo", [P, KT, T], F32R)
        k_stack = sb("k_stack", [98, G, T], F32R)
        q_stack = sb("q_stack", [98, 4, HG, T], F32R)
        v_pad = sb("v_pad", [P, KK, G, 5 * HD])
        nmax = sb("nmax", [P, 2, HG, 2])
        nmax_parts = sb("nmax_parts", [P, 2, 2 * HG * 2], F32R)
        nmax_rows = sb("nmax_rows", [2 * HG * 2, 2, P])
        probs = sb("probs", [P, 2, KK, HG * T])
        o_sb = sb("o_sb", [P, 4, 2, T])

        psP = psum("psP", [P, 2, 512])
        psS = psum("psS", [P, 2, 512])
        psT = psum("psT", [P, 2, 512])
        psO = psum("psO", [P, 2, T])
        psM = psum("psM", [P, P])

        id_landed, filled = sem("id_landed"), sem("filled")
        h_landed, h_hi_done, h_lo_done = sem("h_landed"), sem("h_hi_done"), sem("h_lo_done")
        proj_done = sem("proj_done")
        proj_act, proj_dve = sem("proj_act"), sem("proj_dve")
        k_doubled = sem("k_doubled")
        q_hi_done, q_ready = sem("q_hi_done"), sem("q_ready")
        s_done, s_max = sem("s_done"), sem("s_max")
        nmax_hi, nmax_lo = sem("nmax_hi"), sem("nmax_lo")
        turned, rows_done, rows_landed = sem("turned"), sem("rows_done"), sem("rows_landed")
        st_done, exp_done = sem("st_done"), sem("exp_done")
        pv_done, o_copied = sem("pv_done"), sem("o_copied")
        o_stored = [sem(f"o_stored{i}") for i in range(4)]
        st.proj_done, st.units, st.h_lo_done, st.h_splits = proj_done, NU * B, h_lo_done, 4 * B
        st.pv_done, st.o_copied, st.exp_done = pv_done, o_copied, exp_done
        st.o_stored, st.o_all, st.steps = o_stored, 32 * N // 4, N
        st.proj_act, st.proj_dve, st.s_max = proj_act, proj_dve, s_max

    def live(n):
        return not isinstance(n, int) or 0 <= n < N

    def at(b, unit):
        return NU * b + UNITS.index(unit) + 1

    def has_next(b):
        return not isinstance(b, int) or b < B - 1

    def run(eng, step, peel_last):
        for g in range(G):
            step(g, g, 0)
        with eng.Fori(1, B - 1 if peel_last else B) as b:
            for g in range(G):
                step(G * b + g, g, b)
        if peel_last:
            for g in range(G):
                step(G * (B - 1) + g, g, B - 1)
        for g in range(3):
            step(N + g, g, B)

    def last(n):
        return n - (N - G) if isinstance(n, int) else -1

    def load_h(sp, b):
        sp.dma_start(act_raw[:], hT[bass.ds(b, 1)].rearrange("b p k t -> p (b k t)")).then_inc(h_landed, 16)

    def split_h_hi(act, b, parts):
        if 0 in parts:
            act.wait_ge(h_landed, 16 * b + 16)
            if not isinstance(b, int) or b > 0:
                act.wait_ge(proj_done, NU * b)
        for i in parts:
            cols = slice(i * 512, (i + 1) * 512)
            nc.scalar.activation(h_hi[:, 2 * i:2 * i + 2].rearrange("p k t -> p (k t)"), act_raw[:, cols],
                                 ACT.Copy).then_inc(h_hi_done, 1)

    def split_h_lo(dve, b, parts):
        for i in parts:
            dve.wait_ge(h_hi_done, 4 * b + i + 1)
            cols = slice(i * 512, (i + 1) * 512)
            dve.tensor_tensor(h_lo[:, 2 * i:2 * i + 2].rearrange("p k t -> p (k t)"), act_raw[:, cols],
                              f(h_hi[:, 2 * i:2 * i + 2].rearrange("p k t -> p (k t)")),
                              ALU.subtract).then_inc(h_lo_done, 1)

    def ahead_scalar(act):
        act.wait_ge(before.x_lo_done, before.x_splits)
        split_h_hi(act, 0, range(4))

    def ahead_vector(dve):
        split_h_lo(dve, 0, range(4))

    def ahead_sync(sp):
        for s in before.h_stored:
            sp.wait_ge(s, before.h_all // PAIRS)
        load_h(sp, 0)
        sp.dma_start(id_sb[:], ident).then_inc(id_landed, 16)

    def sync(sp):
        def step(n, g, b):
            if g == 1 and has_next(b):
                sp.wait_ge(h_lo_done, 4 * b + 4)
                load_h(sp, b + 1)
            if live(n - 1):
                sp.wait_ge(rows_done, n)
                r = (g - 1) % 2
                for part in range(2):
                    sp.dma_start(f(q_stack[96 + part:97 + part, (g - 1) % 4].rearrange("p h t -> p (h t)")),
                                 nmax_rows[8 * part:8 * part + 8, r]).then_inc(rows_landed, 16)
            if live(n - 3):
                sp.wait_ge(o_copied, n - 2)
                go, slot = (g - 3) % G, (g - 3) % 4
                bo = b if g >= 3 else b - 1
                ob = oT[bass.ds(bo, 1), :, go].rearrange("b (c p) t -> p (b c) t", c=2)
                sp.dma_start(ob, o_sb[0:64, slot]).then_inc(o_stored[slot], 16)
                db = den[bass.ds(bo, 1), :, go].rearrange("b a c t -> (b a) (c t)")
                sp.dma_start(db, o_sb[64:128:32, slot].rearrange("p c t -> p (c t)")).then_inc(o_stored[slot], 16)
            if last(n) >= 0:
                ahead.sync(sp, last(n))

        for s in before.h_stored:
            sp.wait_ge(s, before.h_all)
        run(sp, step, True)

    def gpsimd(pool):
        pool.wait_ge(before.h_copied, before.tiles)
        for s in before.h_stored:
            pool.wait_ge(s, before.h_all)
        pool.memset(v_pad[:], 0.0).then_inc(filled, 1)
        pool.wait_ge(filled, 1)
        pool.memset(v_pad[:, :, :, 3 * HD:4 * HD], 1.0).then_inc(filled, 1)
        pool.wait_ge(filled, 2)
        pool.memset(f(k_stack[96:98]), 1.0).then_inc(filled, 1)
        for i in range(7, QKV_TILES):
            load_qkv(pool, i)
        for k in range(WO_TILES):
            load_wo(pool, k)

    def scalar(act):
        def copy_k(b, j):
            act.wait_ge(proj_done, at(b, f"k{j}"))
            bank = UNITS.index(f"k{j}") % 2
            for i in range(4):
                ins = nc.scalar.activation(k_stack[0:32, 4 * j + i], psP[32 * i:32 * i + 32, bank, 0:T], ACT.Copy)
            ins.then_inc(proj_act, 1)

        def double_k(b, j):
            act.wait_ge(proj_act, at(b, f"k{j}"))
            nc.scalar.activation(k_stack[32:64, 4 * j:4 * j + 4], k_stack[0:32, 4 * j:4 * j + 4],
                                 ACT.Copy).then_inc(k_doubled, 1)

        def copy_v(b, t):
            act.wait_ge(proj_done, at(b, f"v{t}"))
            v = psP[:, t, 0:NKV].rearrange("p (g d) -> p g d", g=G)
            nc.scalar.activation(v_pad[:, t, 0:4, HD:2 * HD], v[:, 0:4], ACT.Copy).then_inc(proj_act, 1)

        def copy_q(b, g, hp):
            bank = UNITS.index(f"q{g}") % 2
            if hp == 0:
                act.wait_ge(proj_done, at(b, f"q{g}"))
            for h in (2 * hp, 2 * hp + 1):
                ins = nc.scalar.activation(q_stack[0:32, g % 4, h], psP[32 * h:32 * h + 32, bank, 0:T], ACT.Copy)
            ins.then_inc(proj_act if hp else q_hi_done, 1)

        def exp(n, g, i):
            act.wait_ge(st_done, TILES * n + i + 1)
            if i == 0 and live(n - 2):
                act.wait_ge(pv_done, 2 * (n - 1))
            nc.scalar.activation(probs[:, g % 2, i % 2, (i // 2) * 512:(i // 2 + 1) * 512], psT[:, i % 2],
                                 ACT.Exp, scale=ATT_SCALE).then_inc(exp_done, 1)

        def step(n, g, b):
            if isinstance(n, int) and n < G:
                for i in SPLIT_AT[g]:
                    weights.split_hi(act, W_TILES + i, wq[:, i, 0])
            if live(n) and g == 0:
                copy_k(b, 0)
            for hp in range(2):
                if live(n - 2):
                    for i in (2 * hp, 2 * hp + 1):
                        exp(n - 2, g, i)
                if live(n) and hp == 0 and g in (0, 4):
                    double_k(b, g // 4)
                if hp == 1 and live(n - 1):
                    act.wait_ge(turned, n)
                    nc.scalar.activation(nmax_rows[:, (g - 1) % 2], psM[0:16, 0:P], ACT.Copy).then_inc(rows_done, 1)
                if live(n):
                    copy_q(b, g, hp)
                if g == G - 1 and has_next(b):
                    split_h_hi(act, b + 1, (2 * hp, 2 * hp + 1))
            if live(n) and g == 2:
                if live(n - G):
                    act.wait_ge(pv_done, 2 * G * b)
                for t in range(2):
                    copy_v(b, t)
            if live(n) and g == 3:
                copy_k(b, 1)
            if last(n) >= 0:
                ahead.scalar(act, last(n))

        act.wait_ge(filled, 3)
        act.wait_ge(before.h_done, before.tiles)
        run(act, step, True)

    def vector(dve):
        def copy_k(b, j):
            dve.wait_ge(proj_act, at(b, f"k{j}"))
            bank = UNITS.index(f"k{j}") % 2
            for i in range(4):
                kv = 4 * j + i
                ins = dve.tensor_tensor(k_stack[64:96, kv], psP[32 * i:32 * i + 32, bank, 0:T],
                                        f(k_stack[0:32, kv]), ALU.subtract)
            ins.then_inc(proj_dve, 1)

        def copy_v(b, t):
            dve.wait_ge(proj_act, at(b, f"v{t}"))
            v = psP[:, t, 0:NKV].rearrange("p (g d) -> p g d", g=G)
            dve.tensor_copy(v_pad[:, t, 4:8, HD:2 * HD], v[:, 4:8]).then_inc(proj_dve, 1)

        def copy_q(b, n, g, hp):
            bank = UNITS.index(f"q{g}") % 2
            if hp:
                dve.wait_ge(proj_act, at(b, f"q{g}"))
            else:
                dve.wait_ge(q_hi_done, n + 1)
            two = slice(2 * hp, 2 * hp + 2)
            for h in (2 * hp, 2 * hp + 1):
                ins = dve.tensor_tensor(q_stack[32:64, g % 4, h], psP[32 * h:32 * h + 32, bank, 0:T],
                                        f(q_stack[0:32, g % 4, h]), ALU.subtract)
            if hp:
                ins.then_inc(proj_dve, 1)
            dve.tensor_copy(q_stack[64:96, g % 4, two], q_stack[0:32, g % 4, two]).then_inc(q_ready, 1)

        def maxima(n, g, tiles):
            for i in tiles:
                hp, qt = i // 2, i % 2
                dve.wait_ge(s_done, TILES * n + i + 1)
                dve.tensor_reduce(nmax[:, g % 2, 2 * hp:2 * hp + 2, qt],
                                  psS[:, i % 2].rearrange("p (h k) -> p h k", h=2),
                                  AX.X, ALU.max, negate=True).then_inc(s_max, 1)

        def split_maxima(n, g):
            flat = nmax[:, g % 2].rearrange("p h q -> p (h q)")
            dve.wait_ge(s_max, TILES * (n + 1))
            dve.tensor_copy(nmax_parts[:, g % 2, 0:8], flat).then_inc(nmax_hi, 1)
            dve.wait_ge(nmax_hi, n + 1)
            dve.tensor_tensor(nmax_parts[:, g % 2, 8:16], flat, f(nmax_parts[:, g % 2, 0:8]),
                              ALU.subtract).then_inc(nmax_lo, 1)

        def copy_o(n, g, b):
            dve.wait_ge(pv_done, 2 * n + 2)
            if live(n - 4):
                dve.wait_ge(o_stored[g % 4], 32 * (2 * b + g // 4))
            dve.tensor_copy(o_sb[:, g % 4], psO[:]).then_inc(o_copied, 1)

        def step(n, g, b):
            if isinstance(n, int) and n < G:
                for i in SPLIT_AT[g]:
                    weights.split_lo(dve, W_TILES + i, wq[:, i, 0], wq[:, i, 1])
            if live(n - 1):
                maxima(n - 1, (g - 1) % G, (0, 1))
            if live(n) and g in (0, 4):
                copy_k(b, g // 4)
            if live(n - 1):
                maxima(n - 1, (g - 1) % G, (2, 3))
                split_maxima(n - 1, (g - 1) % G)
            for hp in range(2):
                if live(n):
                    copy_q(b, n, g, hp)
                if g == G - 1 and has_next(b):
                    split_h_lo(dve, b + 1, (2 * hp, 2 * hp + 1))
            if live(n - 3):
                copy_o(n - 3, (g - 3) % G, b if g >= 3 else b - 1)
            if live(n) and g == 2:
                for t in range(2):
                    copy_v(b, t)
            if last(n) >= 0:
                ahead.vector(dve, last(n))

        dve.wait_ge(filled, 3)
        run(dve, step, True)

    def tensor(pe):
        def project(b, unit, half=None):
            u = UNITS.index(unit)
            if half in (None, 0) and not (isinstance(b, int) and b == 0 and u < 2):
                pe.wait_ge(proj_act, NU * b + u - 1)
                pe.wait_ge(proj_dve, NU * b + u - 1)
            out = psP[:, u % 2, 0:T]
            kind, j = unit[0], int(unit[1])
            if isinstance(b, int) and b == 0:
                pe.wait_ge(weights.lo_done, W_TILES + (6 if kind == "v" else u + 1))
            for k in range(KT) if half is None else range(4 * half, 4 * half + 4):
                if unit == "k0" and k % 2 == 0:
                    pe.wait_ge(h_lo_done, 4 * b + k // 2 + 1)
                for i, (w, h) in enumerate(((0, h_hi), (0, h_lo), (1, h_hi))):
                    first, end = k == 0 and i == 0, k == KT - 1 and i == 2
                    if kind == "v":
                        mm = pe.matmul(out, h[:, k, j * P:(j + 1) * P], wq[:, 4:6, w, k * P:(k + 1) * P],
                                       start=first, stop=end)
                    else:
                        mm = pe.matmul(out, wq[:, u, w, k * P:(k + 1) * P], h[:, k], start=first, stop=end)
            if half in (None, 1):
                mm.then_inc(proj_done, 1)

        def scores(n, g, i):
            hp, qt = i // 2, i % 2
            if isinstance(n, int) and n == 0 and i == 0:
                pe.wait_ge(before.h_copied, before.tiles)
                pe.wait_ge(filled, 3)
            if qt == 0:
                pe.wait_ge(q_ready, 2 * n + hp + 1)
            if i >= 2 or live(n - 1):
                pe.wait_ge(s_max, TILES * n + i - 1)
            for j in range(2):
                mm = pe.matmul(psS[:, i % 2, j * T:(j + 1) * T],
                               q_stack[0:96, g % 4, 2 * hp + j, qt * P:(qt + 1) * P], k_stack[0:96, g],
                               start=True, stop=True)
            mm.then_inc(s_done, 1)

        def scores_t(n, g, i):
            hp, kt = i // 2, i % 2
            if i == 0:
                pe.wait_ge(rows_landed, 32 * n + 32)
            if i >= 2 or live(n - 1):
                pe.wait_ge(exp_done, TILES * n + i - 1)
            pe.matmul(psT[:, kt], k_stack[0:98, g, kt * P:(kt + 1) * P],
                      q_stack[0:98, g % 4, 2 * hp:2 * hp + 2].rearrange("p h t -> p (h t)"),
                      start=True, stop=True).then_inc(st_done, 1)

        def outputs(n, g, b, hp):
            if hp == 0:
                pe.wait_ge(exp_done, TILES * (n + 1))
                if live(n - 1):
                    pe.wait_ge(o_copied, n)
                if g == 0:
                    pe.wait_ge(proj_act, at(b, "v1"))
                    pe.wait_ge(proj_dve, at(b, "v1"))
            for i in range(2):
                c = HD * (1 - i)
                for kt in range(KK):
                    mm = pe.matmul(psO[:, hp], v_pad[:, kt, g, c:c + P],
                                   probs[:, g % 2, kt, (2 * hp + i) * T:(2 * hp + i + 1) * T],
                                   start=(i == 0 and kt == 0), stop=(i == 1 and kt == 1))
            mm.then_inc(pv_done, 1)

        def turn(n, g):
            pe.wait_ge(nmax_lo, n + 1)
            pe.transpose(psM[0:16, 0:P], f(nmax_parts[:, g % 2]), id_sb[:]).then_inc(turned, 1)

        def step(n, g, b):
            if live(n) and g == 0:
                project(b, "k0")
            for half in range(2):
                if live(n):
                    project(b, f"q{g}", half)
                if live(n - 1):
                    if g == 1 and half == 0:
                        pe.wait_ge(proj_dve, at(b, "k0"))
                        pe.wait_ge(k_doubled, 2 * b + 1)
                    if g == 5 and half == 0:
                        pe.wait_ge(proj_dve, at(b, "k1"))
                        pe.wait_ge(k_doubled, 2 * b + 2)
                    for i in (2 * half, 2 * half + 1):
                        scores(n - 1, (g - 1) % G, i)
            for hp in range(2):
                if live(n - 2):
                    for i in (2 * hp, 2 * hp + 1):
                        scores_t(n - 2, (g - 2) % G, i)
                if hp == 1 and live(n - 1):
                    turn(n - 1, (g - 1) % G)
                if live(n - 3):
                    outputs(n - 3, (g - 3) % G, b, hp)
            if live(n) and g == 2:
                project(b, "v0")
                project(b, "v1")
            if live(n) and g == 3:
                project(b, "k1")

        pe.wait_ge(before.h_copied, before.tiles - 6)
        pe.wait_ge(id_landed, 16)
        run(pe, step, False)

    ahead_here.sync, ahead_here.scalar, ahead_here.vector = ahead_sync, ahead_scalar, ahead_vector
    st.sync, st.gpsimd, st.scalar, st.vector, st.tensor = sync, gpsimd, scalar, vector, tensor
    return st



def finish_stage(nc, sem, weights, wq, o_raw, o_scale, den_sb, ra_raw, id_sb, idx_sb, before, ahead,
                 xT, oT, den, rden, idx, cond2, RA, ffn_B, outT):
    RAW, SPLIT = 4, 2
    ROWS_AT = [[0], [1], [2], [3], [4], [5], [6, 7], []]
    YT = KT // 2
    BN = 2 * G * 2 * T // P
    HEAD = B - 1
    CH = 16
    st = Stage()
    with ExitStack() as ctx:
        def sb(name, shape, dt=F32):
            return ctx.enter_context(nc.sbuf_tensor(name, shape, dt))

        def psum(name, shape):
            return ctx.enter_context(nc.psum_tensor(name, shape, F32))

        sb("weights_all", [P, QKV_TILES, 2, D])
        cond_raw = sb("cond_raw", [P, RAW, D])
        cond_hi, cond_lo = sb("cond_hi", [P, SPLIT, D], F32R), sb("cond_lo", [P, SPLIT, D], F32R)
        ra_hi, ra_lo = sb("ra_hi", [P, KT, EC], F32R), sb("ra_lo", [P, KT, EC], F32R)
        x_sb = sb("x_sb", [P, 2, KT, T])
        g_sb = sb("g_sb", [EC, D])
        fb_raw = sb("fb_raw", [P, D])
        fb_stack = sb("fb_stack", [P, D], F32R)
        g_t = sb("g_t", [P, KT, EC])
        mid = sb("mid", [P, 2, EC])
        rank0, rank, beats = (sb(name, [P, 2, E]) for name in ("rank0", "rank", "beats"))
        gate = sb("gate", [P, 2, E])
        top, gsum = sb("top", [P, 2]), sb("gsum", [P, 2])
        gated = sb("gated", [P, 2, P])
        gated_hi, gated_lo = sb("gated_hi", [P, T], F32R), sb("gated_lo", [P, T], F32R)

        psW = psum("psW", [P, 2, 512])
        psG = psum("psG", [P, 2, 512])
        psY = psum("psY", [P, 2, 512])
        psX = psum("psX", [P, 2, 512])

        const_landed, fb_landed = sem("const_landed"), sem("fb_landed")
        den_landed, rden_done, rden_stored = sem("den_landed"), sem("rden_done"), sem("rden_stored")
        o_landed, x_landed = sem("o_landed"), [sem(f"x_landed_{c}") for c in range(2)]
        o_scaled, o_hi_done, o_lo_done = sem("o_scaled"), sem("o_hi_done"), sem("o_lo_done")
        wo_done, x2_done = sem("wo_done"), sem("x2_done")
        cond_landed = [sem(f"cond_landed{i}") for i in range(RAW)]
        cond_hi_done, cond_lo_done, cond_used = sem("cond_hi_done"), sem("cond_lo_done"), sem("cond_used")
        ra_hi_done, ra_lo_done = sem("ra_hi_done"), sem("ra_lo_done")
        fb_hi_done, fb_lo_done = sem("fb_hi_done"), sem("fb_lo_done")
        g_copied = sem("g_copied")
        gt_done, gt_copied = sem("gt_done"), sem("gt_copied")
        mid_done = sem("mid_done")
        chain = sem("chain")
        shifted, gate_exp = sem("shifted"), sem("gate_exp")
        gated_done, gated_turned = sem("gated_done"), sem("gated_turned")
        gated_hi_done, gated_lo_done = sem("gated_hi_done"), sem("gated_lo_done")
        y_done, y_added = sem("y_done"), sem("y_added")
        stored = sem("stored")

    def o_part(c, part):
        return wq[:, 8 + 2 * c + part].rearrange("p w (k t) -> p (w k) t", t=T)

    def run(batch):
        def program(eng):
            for n in range(2):
                batch(n, n)
            with eng.Fori(1, PAIRS - 1) as pair:
                for c in range(2):
                    batch(2 * pair + c, c)
            for c in range(2):
                batch(B - 2 + c, c)
        return program

    def is_first(n):
        return isinstance(n, int) and n == 0

    def is_last(n):
        return isinstance(n, int) and n == B - 1

    def spread(d, first, count):
        return d[first:first + count].rearrange("b c g h t -> b (c g h t)").rearrange("b (p n) -> p b n", p=P)

    den_view = den_sb[:].rearrange("p (b n) -> p b n", b=B)

    def load_o(sp, n):
        srcs = [rden[bass.ds(n, 1), h % 2, :, h // 2].to_broadcast([32, G, T]) for h in range(HG)]
        src = oT[bass.ds(n, 1)].rearrange("b p g t -> p (b g t)")
        if not is_first(n):
            sp.wait_ge(o_lo_done, n)
        sp.dma_start(o_raw[:], src).then_inc(o_landed, 16)
        for h in range(HG):
            sp.dma_start(o_scale[32 * h:32 * h + 32], srcs[h]).then_inc(o_landed, 16)

    def ahead_sync(sp, s):
        if s == 0:
            sp.dma_start(ra_raw[:], RA).then_inc(const_landed, 16)
            sp.dma_start(idx_sb[:], idx).then_inc(const_landed, 16)
        if s == 4:
            for i in range(4):
                sp.wait_ge(before.o_stored[i], before.o_all // B * HEAD)
            sp.dma_start(den_view[:, 0:HEAD], spread(den, 0, HEAD)).then_inc(den_landed, 16)
        if s == 6:
            sp.wait_ge(rden_done, 1)
            sp.dma_start(spread(rden, 0, HEAD), den_view[:, 0:HEAD]).then_inc(rden_stored, 16)
        if s == 7:
            sp.wait_ge(rden_stored, 16)
            load_o(sp, 0)

    def load_x(sp, n, c):
        sp.dma_start(x_sb[:, c], xT[bass.ds(n, 1)].rearrange("b p k t -> p (b k) t")).then_inc(x_landed[c], 16)

    def sync(sp):
        def store(n, c, value):
            dst = outT[bass.ds(n, 1)].rearrange("b p k t -> p (b k) t")
            sp.wait_ge(y_added, value)
            sp.dma_start(dst, x_sb[:, c]).then_inc(stored, 16)

        def batch(n, c):
            if not is_last(n):
                load_o(sp, n + 1)
            if not is_first(n):
                store(n - 1, 1 - c, YT * n)
                if not is_last(n):
                    sp.wait_ge(stored, 16 * n)
                    load_x(sp, n + 1, 1 - c)
            else:
                sp.wait_ge(rden_done, 2)
                sp.dma_start(spread(rden, HEAD, 1), den_view[:, HEAD:B]).then_inc(rden_stored, 16)
                sp.wait_ge(rden_stored, 32)

        sp.wait_ge(before.pv_done, 2 * before.steps)
        load_x(sp, 0, 0)
        load_x(sp, 1, 1)
        for s in before.o_stored:
            sp.wait_ge(s, before.o_all)
        sp.dma_start(den_view[:, HEAD:B], spread(den, HEAD, 1)).then_inc(den_landed, 16)
        for half in range(2):
            sp.dma_start(fb_raw[ER * half:ER * (half + 1)], ffn_B).then_inc(fb_landed, 16)
        run(batch)(sp)
        store(B - 1, 1, YT * B)
        sp.wait_ge(stored, 16 * B)

    def gpsimd(pool):
        def row(n_row, slot, k):
            pool.dma_start(cond_raw[:, k % RAW], cond2[bass.ds(slot, 1), k].rearrange("s p d -> (s p) d")
                           ).then_inc(cond_landed[k % RAW], 16)

        def batch(n, c):
            slot = pool.value_load(idx_sb[0:1, bass.ds(n, 1)], min_val=0, max_val=7)
            for k in range(RAW, KT):
                pool.wait_ge(cond_lo_done, KT * n + k - RAW + 1)
                row(n, slot, k)
            if not is_last(n):
                slot = pool.value_load(idx_sb[0:1, bass.ds(n + 1, 1)], min_val=0, max_val=7)
                for k in range(RAW):
                    pool.wait_ge(cond_lo_done, KT * n + KT - RAW + k + 1)
                    row(n, slot, k)

        pool.wait_ge(const_landed, 32)
        slot = pool.value_load(idx_sb[0:1, 0:1], min_val=0, max_val=7)
        pool.wait_ge(before.proj_done, before.units)
        for k in range(RAW):
            row(0, slot, k)
        run(batch)(pool)

    def scale_hi(act, n, c):
        act.wait_ge(o_scaled, n + 1)
        if not (isinstance(n, int) and n < 2):
            act.wait_ge(wo_done, KT * (n - 1))
        nc.scalar.activation(o_part(c, 0), o_raw[:].rearrange("p (k t) -> p k t", t=T),
                             ACT.Copy).then_inc(o_hi_done, 1)

    def ahead_scalar(act, s):
        if 4 <= s < 8:
            act.wait_ge(before.proj_done, before.units - 4)
            for k in (2 * (s - 4), 2 * (s - 4) + 1):
                weights.split_hi(act, W_TILES + QKV_TILES + k, wq[:, k, 0])
        if s == 8:
            act.wait_ge(before.proj_done, before.units)
            scale_hi(act, 0, 0)

    def scalar(act):
        def cond_row(n, k):
            act.wait_ge(cond_landed[k % RAW], 16 * (2 * n + k // RAW + 1))
            if not (is_first(n) and k < SPLIT):
                act.wait_ge(cond_used, KT * n + k - SPLIT + 1)
            nc.scalar.activation(cond_hi[:, k % SPLIT], cond_raw[:, k % RAW], ACT.Copy).then_inc(cond_hi_done, 1)

        def gates(n):
            act.wait_ge(shifted, n)
            nc.scalar.activation(gate[:], beats[:], ACT.Exp).then_inc(gate_exp, 1)

        def gated_part(n):
            act.wait_ge(gated_turned, n)
            nc.scalar.activation(gated_hi[:], psX[:, 1, 0:T], ACT.Copy, scale=FFN_SCALE).then_inc(gated_hi_done, 1)

        def batch(n, c):
            if is_first(n):
                nc.scalar.activation(ra_hi[:], ra_raw[:], ACT.Copy).then_inc(ra_hi_done, 1)
                cond_row(n, 0)
                cond_row(n, 1)
            else:
                gates(n)
            cond_row(n, 2)
            cond_row(n, 3)
            if not is_first(n):
                gated_part(n)
            for k in (4, 5, 6, 7):
                cond_row(n, k)
            if not is_last(n):
                scale_hi(act, n + 1, 1 - c)
            if is_first(n):
                act.wait_ge(fb_landed, 32)
                nc.scalar.activation(fb_stack[:], fb_raw[:], ACT.Copy).then_inc(fb_hi_done, 1)
            act.wait_ge(cond_used, KT * (n + 1))
            nc.scalar.activation(g_sb[:], psG[0:EC].rearrange("p a b -> p (a b)"), ACT.Copy).then_inc(g_copied, 1)
            if not is_last(n):
                cond_row(n, 8)
                cond_row(n, 9)

        act.wait_ge(const_landed, 32)
        act.wait_ge(before.pv_done, 2 * before.steps)
        run(batch)(act)
        gates(B)
        gated_part(B)

    def scale_o(dve, n):
        dve.wait_ge(o_landed, 16 * (1 + HG) * (n + 1))
        dve.tensor_tensor(o_raw[:], o_raw[:], o_scale[:].rearrange("p g t -> p (g t)"), ALU.mult).then_inc(o_scaled, 1)

    def scale_lo(dve, n, c):
        dve.wait_ge(o_hi_done, n + 1)
        dve.tensor_tensor(o_part(c, 1), o_raw[:].rearrange("p (k t) -> p k t", t=T), f(o_part(c, 0)),
                          ALU.subtract).then_inc(o_lo_done, 1)

    def invert(dve, first, count):
        part = den_sb[:, first * BN:(first + count) * BN]
        dve.reciprocal(part, part).then_inc(rden_done, 1)

    def ahead_vector(dve, s):
        if s == 5:
            dve.wait_ge(den_landed, 16)
            invert(dve, 0, HEAD)
        if 4 <= s < 8:
            for k in (2 * (s - 4), 2 * (s - 4) + 1):
                weights.split_lo(dve, W_TILES + QKV_TILES + k, wq[:, k, 0], wq[:, k, 1])
        if s == 8:
            scale_o(dve, 0)
        if s == 9:
            scale_lo(dve, 0, 0)

    def vector(dve):
        def cond_row(n, k):
            dve.wait_ge(cond_hi_done, KT * n + k + 1)
            dve.tensor_tensor(cond_lo[:, k % SPLIT], cond_raw[:, k % RAW], f(cond_hi[:, k % SPLIT]),
                              ALU.subtract).then_inc(cond_lo_done, 1)

        def residual(n, c, m):
            if m == 0:
                dve.wait_ge(x_landed[c], 16 * (n // 2 + 1) if isinstance(n, int) else 8 * (n - c) + 16)
            dve.wait_ge(wo_done, KT * n + m + 1)
            dve.tensor_tensor(x_sb[:, c, m], x_sb[:, c, m], psW[:, m % 2, 0:T], ALU.add).then_inc(x2_done, 1)

        def gates(n):
            done = [0]

            def step(ins):
                done[0] += 1
                ins.then_inc(chain, 1)
                dve.wait_ge(chain, CH * (n - 1) + done[0] + 1)

            dve.wait_ge(mid_done, n)
            step(dve.tensor_copy(mid[:], psX[:, 0, 0:2 * EC].rearrange("p (t e) -> p t e", t=2)))
            logit = mid[:, :, ER:EC]
            step(dve.tensor_reduce(top[:], logit, AX.X, ALU.max))
            for t in range(2):
                ins = dve.tensor_scalar(beats[:, t], logit[:, t], top[:, t:t + 1], None, ALU.subtract)
            ins.then_inc(shifted, 1)
            dve.wait_ge(gate_exp, n)
            for d in range(1, E):
                step(dve.tensor_tensor(beats[:, :, 0:E - d], logit[:, :, d:E], logit[:, :, 0:E - d], ALU.is_gt))
                if d == 1:
                    step(dve.tensor_copy(rank[:], rank0[:]))
                step(dve.tensor_tensor(rank[:, :, 0:E - d], rank[:, :, 0:E - d], beats[:, :, 0:E - d], ALU.add))
                step(dve.tensor_tensor(rank[:, :, d:E], rank[:, :, d:E], beats[:, :, 0:E - d], ALU.subtract))
            step(dve.scalar_tensor_tensor(gate[:], rank[:], 1.5, gate[:], ALU.is_lt, ALU.mult))
            step(dve.tensor_reduce(gsum[:], gate[:], AX.X, ALU.add))
            step(dve.reciprocal(gsum[:], gsum[:]))
            for t in range(2):
                for e in range(E):
                    ins = dve.tensor_scalar(gated[:, t, e * R:(e + 1) * R], mid[:, t, e * R:(e + 1) * R],
                                            gate[:, t, e:e + 1], gsum[:, t:t + 1], ALU.mult, ALU.mult)
            step(ins)
            assert done[0] == CH
            dve.tensor_copy(gated[:, :, ER:2 * ER], gated[:, :, 0:ER]).then_inc(gated_done, 1)

        def gated_part(n):
            dve.wait_ge(gated_hi_done, n)
            dve.scalar_tensor_tensor(gated_lo[:], psX[:, 1, 0:T], FFN_SCALE, f(gated_hi[:]),
                                     ALU.mult, ALU.subtract).then_inc(gated_lo_done, 1)

        def add_y(n, c, j):
            dve.wait_ge(y_done, YT * (n - 1) + j + 1)
            dve.tensor_tensor(x_sb[:, c, 2 * j:2 * j + 2], x_sb[:, c, 2 * j:2 * j + 2],
                              psY[:, j % 2].rearrange("p (m t) -> p m t", m=2), ALU.add).then_inc(y_added, 1)

        def batch(n, c):
            if is_first(n):
                dve.wait_ge(ra_hi_done, 1)
                dve.tensor_tensor(ra_lo[:], ra_raw[:], f(ra_hi[:]), ALU.subtract).then_inc(ra_lo_done, 1)
                cond_row(n, 0)
                cond_row(n, 1)
            else:
                gates(n)
            for m in range(KT):
                if m == 7:
                    for half in range(2):
                        dve.wait_ge(gt_done, 2 * n + half + 1)
                        dve.tensor_copy(g_t[:, 4 * half:4 * half + 4],
                                        psX[:, half, 0:4 * EC].rearrange("p (k e) -> p k e", k=4)).then_inc(gt_copied, 1)
                residual(n, c, m)
                if m < 6:
                    cond_row(n, m + 2)
                if is_first(n):
                    if m == 1:
                        for s in before.o_stored:
                            dve.wait_ge(s, before.o_all)
                        for e in range(E):
                            ins = dve.memset(rank0[:, :, e:e + 1], float(e))
                        ins.then_inc(chain, 1)
                        dve.wait_ge(den_landed, 32)
                        invert(dve, HEAD, 1)
                else:
                    if m == 1:
                        gated_part(n)
                    if m in (2, 3):
                        add_y(n, 1 - c, 2 * (m - 2))
                        add_y(n, 1 - c, 2 * (m - 2) + 1)
                if m == 4 and not is_last(n):
                    scale_o(dve, n + 1)
                if m == 6 and not is_last(n):
                    scale_lo(dve, n + 1, 1 - c)
                if m == 6 and is_first(n):
                    dve.wait_ge(fb_hi_done, 1)
                    dve.tensor_tensor(fb_stack[ER:P], fb_raw[ER:P], f(fb_stack[ER:P]),
                                      ALU.subtract).then_inc(fb_lo_done, 1)
            if not is_last(n):
                cond_row(n, 8)
                cond_row(n, 9)

        run(batch)(dve)
        gates(B)
        gated_part(B)
        for j in range(YT):
            add_y(B, 1, j)

    def tensor(pe):
        def w_o_tile(n, c, m, ks):
            out = psW[:, m % 2, 0:T]
            if ks[0] == 0:
                if is_first(n) and m < 2:
                    pe.wait_ge(before.proj_act, before.units)
                    pe.wait_ge(before.proj_dve, before.units)
                else:
                    pe.wait_ge(x2_done, KT * n + m - 1)
            for k in ks:
                for i, (w, o) in enumerate(((0, 0), (0, 1), (1, 0))):
                    mm = pe.matmul(out, wq[:, k, w, m * P:(m + 1) * P], o_part(c, o)[:, k],
                                   start=(k == 0 and i == 0), stop=(k == KT - 1 and i == 2))
            if ks[-1] == KT - 1:
                mm.then_inc(wo_done, 1)

        def cond_row(n, k):
            pe.wait_ge(cond_lo_done, KT * n + k + 1)
            if k == 0:
                if is_first(n):
                    pe.wait_ge(ra_lo_done, 1)
                    pe.wait_ge(before.s_max, 4 * before.steps)
                else:
                    pe.wait_ge(g_copied, n)
            for i, (a, w) in enumerate(((ra_hi, cond_hi), (ra_hi, cond_lo), (ra_lo, cond_hi))):
                for half in range(2):
                    mm = pe.matmul(psG[0:EC, half], a[:, k], w[:, k % SPLIT, half * 512:(half + 1) * 512],
                                   start=(k == 0 and i == 0), stop=(k == KT - 1 and i == 2))
            mm.then_inc(cond_used, 1)

        def turn_g(n):
            if is_first(n):
                pe.wait_ge(before.o_copied, before.steps)
            pe.wait_ge(g_copied, n + 1)
            for half in range(2):
                for k in range(4):
                    kk = 4 * half + k
                    mm = pe.transpose(psX[:, half, k * EC:(k + 1) * EC], g_sb[:, kk * P:(kk + 1) * P],
                                      id_sb[0:EC, 0:EC])
                mm.then_inc(gt_done, 1)

        def middle(n, c):
            pe.wait_ge(gt_copied, 2 * n + 2)
            for t in range(2):
                for k in range(KT):
                    if t == 0 and k == KT - 1:
                        pe.wait_ge(x2_done, KT * (n + 1))
                    mm = pe.matmul(psX[:, 0, t * EC:(t + 1) * EC], x_sb[:, c, k, t * P:(t + 1) * P], g_t[:, k],
                                   start=(k == 0), stop=(k == KT - 1))
            mm.then_inc(mid_done, 1)

        def turn_gated(n):
            pe.wait_ge(gated_done, n)
            for t in range(2):
                mm = pe.transpose(psX[:, 1, t * P:(t + 1) * P], gated[:, t], id_sb[:])
            mm.then_inc(gated_turned, 1)

        def y_tile(n, j):
            if j == 0:
                pe.wait_ge(gated_lo_done, n)
                if isinstance(n, int) and n == 1:
                    pe.wait_ge(fb_lo_done, 1)
            if j >= 2 or not (isinstance(n, int) and n == 1):
                pe.wait_ge(y_added, YT * (n - 1) + j - 1)
            for m in (2 * j, 2 * j + 1):
                for i, g in enumerate((gated_hi, gated_lo)):
                    mm = pe.matmul(psY[:, j % 2, (m % 2) * T:(m % 2 + 1) * T], fb_stack[:, m * P:(m + 1) * P], g[:],
                                   start=(i == 0), stop=(i == 1))
            mm.then_inc(y_done, 1)

        def batch(n, c):
            pe.wait_ge(o_lo_done, n + 1)
            for m in range(KT):
                if m == 7:
                    w_o_tile(n, c, m, range(4))
                    turn_g(n)
                    w_o_tile(n, c, m, range(4, KT))
                else:
                    w_o_tile(n, c, m, range(KT))
                for k in ROWS_AT[m]:
                    cond_row(n, k)
                if not is_first(n):
                    if m == 1:
                        turn_gated(n)
                    if m in (2, 3):
                        y_tile(n, 2 * (m - 2))
                        y_tile(n, 2 * (m - 2) + 1)
            middle(n, c)

        pe.wait_ge(weights.lo_done, W_TILES + QKV_TILES + WO_TILES)
        pe.wait_ge(const_landed, 32)
        run(batch)(pe)
        turn_gated(B)
        for j in range(YT):
            y_tile(B, j)

    ahead.sync, ahead.scalar, ahead.vector = ahead_sync, ahead_scalar, ahead_vector
    st.sync, st.gpsimd, st.scalar, st.vector, st.tensor = sync, gpsimd, scalar, vector, tensor
    return st


_INS = ["xT", "itok_A", "itok_C", "WT", "bias", "lora_A", "lora_B", "Wqkv", "Wo", "cond2", "RA", "ffn_B", "ident"]


def build(nc, a, outT):
    hT = nc.dram_tensor("h_scratch", (B, P, KT, T), F32).ap()
    oT = nc.dram_tensor("o_scratch", (B, P, G, T), F32).ap()
    den = nc.dram_tensor("den_scratch", (B, 2, G, 2, T), F32).ap()
    rden = nc.dram_tensor("rden_scratch", (B, 2, G, 2, T), F32).ap()
    COLS = [D, 0, P, 2 * P, D + NKV, D + NKV + P, 3 * P, D + P, 4 * P, 5 * P, 6 * P, 7 * P]

    def load_qkv(eng, i):
        weights.load(eng, W_TILES + i, a["Wqkv"][:, COLS[i]:COLS[i] + P].rearrange("(k p) c -> p k c", p=P))

    def load_wo(eng, k):
        weights.load(eng, W_TILES + QKV_TILES + k, a["Wo"][k * P:(k + 1) * P])

    with ExitStack() as ctx:
        def sb(name, shape, dt=F32):
            return ctx.enter_context(nc.sbuf_tensor(name, shape, dt))

        def sem(name):
            return ctx.enter_context(nc.semaphore(name))

        weights = Weights(nc, sb, sem)
        act_raw = sb("act_raw", [P, KT * T])
        o_scale = sb("o_scale", [P, G, T])
        den_sb = sb("den_sb", [P, B * 2 * G * 2 * T // P])
        ra_raw = sb("ra_raw", [P, KT, EC])
        id_sb = sb("id_sb", [P, P])
        wb_idx = sb("wb_idx", [1, B], I32)
        ahead_attend, ahead_finish = Stage(), Stage()
        with nc.sbuf_tensor("wq", [P, QKV_TILES, 2, D], F32R) as wq:
            pass
        tokens = tokens_stage(nc, sem, weights, wq, ahead_attend, load_qkv, a["xT"], a["itok_A"], a["WT"], a["bias"],
                              a["lora_A"], a["lora_B"], hT)
        attend = attend_stage(nc, sem, weights, wq, act_raw, load_qkv, load_wo, tokens, ahead_attend,
                              ahead_finish, id_sb, a["ident"], hT, oT, den)
        finish = finish_stage(nc, sem, weights, wq, act_raw, o_scale, den_sb, ra_raw, id_sb, wb_idx, attend,
                              ahead_finish, a["xT"], oT, den, rden, a["itok_C"], a["cond2"], a["RA"], a["ffn_B"], outT)
        with nc.Block() as block:
            @block.sync
            def _(sp):
                tokens.sync(sp)
                attend.sync(sp)
                finish.sync(sp)

            @block.gpsimd
            def _(pool):
                tokens.gpsimd(pool)
                attend.gpsimd(pool)
                finish.gpsimd(pool)

            @block.scalar
            def _(act):
                tokens.scalar(act)
                attend.scalar(act)
                finish.scalar(act)

            @block.vector
            def _(dve):
                tokens.vector(dve)
                attend.vector(dve)
                finish.vector(dve)

            @block.tensor
            def _(pe):
                tokens.tensor(pe)
                attend.tensor(pe)
                finish.tensor(pe)


def kernel(x, itok_B_0_23, itok_B_3_7, L0_cond_W, L0_cond_b, L0_cond_lora_As, L0_cond_lora_Bs, L0_attn_w_q,
           L0_attn_w_k, L0_attn_w_v, L0_attn_w_o, L0_cond2_weight, L0_ffn_router_w, L0_ffn_A, L0_ffn_B):
    import concourse.bacc as _bacc
    from concourse.bass_utils import run_bass_kernel_spmd as _run

    def tiles(a):
        a = a.reshape(a.shape[:-2] + (KT, P, a.shape[-1]))
        return np.swapaxes(a, -3, -2)

    x = np.asarray(x)
    arrays = {
        "xT": tiles(np.swapaxes(x, 1, 2)),
        "itok_A": np.asarray(itok_B_0_23).reshape(1, B),
        "itok_C": np.asarray(itok_B_3_7).reshape(1, B),
        "WT": tiles(np.asarray(L0_cond_W).T),
        "bias": np.asarray(L0_cond_b).reshape(KT, P).T,
        "lora_A": tiles(np.asarray(L0_cond_lora_As)),
        "lora_B": np.asarray(L0_cond_lora_Bs),
        "Wqkv": np.concatenate([np.asarray(w) for w in (L0_attn_w_q, L0_attn_w_k, L0_attn_w_v)], axis=1),
        "Wo": np.asarray(L0_attn_w_o),
        "cond2": np.asarray(L0_cond2_weight).reshape(-1, KT, P, D),
        "RA": tiles(np.concatenate([np.asarray(L0_ffn_A).reshape(ER, D), np.asarray(L0_ffn_router_w)], axis=0).T),
        "ffn_B": np.swapaxes(np.asarray(L0_ffn_B), 1, 2).reshape(ER, D),
        "ident": np.eye(P, dtype=np.float32),
    }
    nc = _bacc.Bacc("TRN2", target_bir_lowering=False, num_devices=1)
    aps, sent = {}, {}
    for name in _INS:
        v = np.ascontiguousarray(arrays[name])
        sent[f"in_{name}"] = v
        aps[name] = nc.dram_tensor(f"in_{name}", v.shape, mybir.dt.from_np(v.dtype), kind="ExternalInput").ap()
    outT = nc.dram_tensor("outT", (B, P, KT, T), F32, kind="ExternalOutput").ap()
    build(nc, aps, outT)
    r = _run(nc, [sent], core_ids=[0])
    out = r.results[0]["outT"]
    return np.ascontiguousarray(out.transpose(0, 3, 2, 1).reshape(B, T, D))
```
